# Optimizing a Trainium2 kernel written in Bass

```python
import numpy as np
import jax
import jax.numpy as jnp

def _softmax(x, axis=-1):
    return jax.nn.softmax(x, axis=axis)

def _gelu(x):
    return jax.nn.gelu(x, approximate=True)

def _silu(x):
    return jax.nn.silu(x)

def _sigmoid(x):
    return jax.nn.sigmoid(x)

def _layernorm(x, axis=-1, eps=1e-05):
    m = jnp.mean(x, axis=axis, keepdims=True)
    v = jnp.var(x, axis=axis, keepdims=True)
    return (x - m) / jnp.sqrt(v + eps)

def _scatter_add(tgt, idx, src, axis=0):
    return tgt.at[idx].add(src)

def _segment_sum(src, seg, n):
    return jax.ops.segment_sum(src, seg, n)
kernel_name = 'mk_audio_tower_d1_tok_aud1d1024_r4_de934d'

def setup_inputs(seed: int=0):
    np.random.seed(seed)
    _w = jnp.asarray

    def _rec_inputs():
        import jax
        import jax.numpy as jnp
        _rk = jax.random.key(seed)
        x = -0.000296005 + 1.00001 * jax.random.normal(jax.random.fold_in(_rk, 1), (2, 327680), jnp.float32)
        return x
    x = _rec_inputs()

    def _L0_tok_setup():
        import jax, jax.numpy as jnp
        import numpy as np
        RF = 80
        HID = 256
        LN_EPS = 1e-05
        key = jax.random.key(seed)
        k1, k2, k3, k4, k5 = jax.random.split(key, 5)
        waveform = jax.random.normal(k1, (16, 327680), dtype=jnp.float32)
        bound = 1.0 / np.sqrt(RF)
        W = jax.random.uniform(k2, (HID, RF), dtype=jnp.float32, minval=-bound, maxval=bound)
        b = jax.random.uniform(k3, (HID,), dtype=jnp.float32, minval=-bound, maxval=bound)
        ln_gamma = jnp.ones((HID,), dtype=jnp.float32)
        ln_beta = jnp.zeros((HID,), dtype=jnp.float32)
        return {'waveform': waveform, 'W': W, 'b': b, 'ln_gamma': ln_gamma, 'ln_beta': ln_beta}
    _L0_tok_all = _L0_tok_setup()
    _L0_tok_in = {k: v for k, v in _L0_tok_all.items() if k in ('W', 'b', 'ln_gamma', 'ln_beta')}
    del _L0_tok_all

    def _L0_attn_setup():
        import jax, jax.numpy as jnp
        import numpy as np
        H = 16
        NB = 64
        NH = 6
        key = jax.random.key(seed)
        k = jax.random.split(key, 6)
        E = 256
        B, S = (2, 512)
        return {'x': jax.random.normal(k[0], (B, S, E), jnp.float32), 'Wq': jax.random.normal(k[1], (E, E), jnp.float32) * E ** (-0.5), 'bq': jax.random.normal(k[2], (E,), jnp.float32) * 0.02, 'Wv': jax.random.normal(k[3], (E, E), jnp.float32) * E ** (-0.5), 'bv': jax.random.normal(k[4], (E,), jnp.float32) * 0.02, 'hyperplanes': jax.random.normal(k[5], (E // H + 1, NH), jnp.float32)}
    _L0_attn_all = _L0_attn_setup()
    _L0_attn_in = {k: v for k, v in _L0_attn_all.items() if k in ('Wq', 'bq', 'Wv', 'bv', 'hyperplanes')}
    del _L0_attn_all

    def _L0_ffn_setup():
        import jax, jax.numpy as jnp
        import numpy as np
        B, S, D, O, E, R, TOP_K = (4, 256, 256, 256, 8, 16, 2)
        SCALING = 32.0 / 16.0
        NEG_INF = -1000000000.0
        key = jax.random.key(seed)
        ks = jax.random.split(key, 6)
        return {'x': jax.random.normal(ks[0], (B, S, D), jnp.float32), 'base_w': jax.random.normal(ks[1], (O, D), jnp.float32) * 0.02, 'base_b': jnp.zeros((O,), jnp.float32), 'lora_A': jax.random.normal(ks[2], (E, D, R), jnp.float32) * 0.02, 'lora_B': jax.random.normal(ks[3], (E, R, O), jnp.float32) * 0.02, 'router_w': jax.random.normal(ks[4], (E, D), jnp.float32) * 0.02, 'router_b': jnp.zeros((E,), jnp.float32)}
    _L0_ffn_all = _L0_ffn_setup()
    _L0_ffn_in = {k: v for k, v in _L0_ffn_all.items() if k in ('base_w', 'base_b', 'lora_A', 'lora_B', 'router_w', 'router_b')}
    del _L0_ffn_all
    return {'x': x, 'L0_tok_W': _L0_tok_in['W'], 'L0_tok_b': _L0_tok_in['b'], 'L0_tok_ln_gamma': _L0_tok_in['ln_gamma'], 'L0_tok_ln_beta': _L0_tok_in['ln_beta'], 'L0_attn_Wq': _L0_attn_in['Wq'], 'L0_attn_bq': _L0_attn_in['bq'], 'L0_attn_Wv': _L0_attn_in['Wv'], 'L0_attn_bv': _L0_attn_in['bv'], 'L0_attn_hyperplanes': _L0_attn_in['hyperplanes'], 'L0_ffn_base_w': _L0_ffn_in['base_w'], 'L0_ffn_base_b': _L0_ffn_in['base_b'], 'L0_ffn_lora_A': _L0_ffn_in['lora_A'], 'L0_ffn_lora_B': _L0_ffn_in['lora_B'], 'L0_ffn_router_w': _L0_ffn_in['router_w'], 'L0_ffn_router_b': _L0_ffn_in['router_b']}

def reference(x, L0_tok_W, L0_tok_b, L0_tok_ln_gamma, L0_tok_ln_beta, L0_attn_Wq, L0_attn_bq, L0_attn_Wv, L0_attn_bv, L0_attn_hyperplanes, L0_ffn_base_w, L0_ffn_base_b, L0_ffn_lora_A, L0_ffn_lora_B, L0_ffn_router_w, L0_ffn_router_b):
    import jax
    import jax.numpy as jnp

    def _L0_tok_ref(waveform, W, b, ln_gamma, ln_beta):
        import jax, jax.numpy as jnp
        import numpy as np
        RF = 80
        HID = 256
        LN_EPS = 1e-05
        B, T = waveform.shape
        x = waveform.reshape(B, T // RF, RF)
        h = jnp.einsum('bfr,hr->bfh', x, W) + b
        mu = jnp.mean(h, axis=-1, keepdims=True)
        var = jnp.mean(jnp.square(h - mu), axis=-1, keepdims=True)
        h = (h - mu) * jax.lax.rsqrt(var + LN_EPS) * ln_gamma + ln_beta
        return h * 0.5 * (1.0 + jax.lax.erf(h / jnp.sqrt(jnp.float32(2.0))))

    def _L0_attn_ref(x, Wq, bq, Wv, bv, hyperplanes):
        import jax, jax.numpy as jnp
        import numpy as np
        H = 16
        NB = 64
        NH = 6
        B, S, E = x.shape
        Dh = E // H
        q = (x @ Wq.T + bq).reshape(B, S, H, Dh)
        v = (x @ Wv.T + bv).reshape(B, S, H, Dh)
        qa = jnp.concatenate([q, jnp.ones((B, S, H, 1), q.dtype)], axis=-1)
        proj = jnp.einsum('bshe,en->bshn', qa, hyperplanes)
        bits = (proj >= 0).astype(jnp.int32)
        buckets = jnp.einsum('bshn,n->bsh', bits, 2 ** jnp.arange(NH, dtype=jnp.int32))
        b_hs = buckets.transpose(0, 2, 1)
        q = q.transpose(0, 2, 1, 3)
        v = v.transpose(0, 2, 1, 3)
        scores = jnp.einsum('bhsd,bhtd->bhst', q, q) / jnp.sqrt(jnp.float32(E))
        same = (b_hs[:, :, :, None] == b_hs[:, :, None, :]).astype(scores.dtype)
        coeff = NB - 2 + same
        attn = jax.nn.softmax(scores * coeff, axis=-1)
        out = jnp.einsum('bhst,bhtd->bhsd', attn, v)
        return out.transpose(0, 2, 1, 3).reshape(B, S, E)

    def _L0_ffn_ref(x, base_w, base_b, lora_A, lora_B, router_w, router_b):
        import jax, jax.numpy as jnp
        import numpy as np
        B, S, D, O, E, R, TOP_K = (4, 256, 256, 256, 8, 16, 2)
        SCALING = 32.0 / 16.0
        NEG_INF = -1000000000.0
        result = jnp.einsum('bsd,od->bso', x, base_w) + base_b
        ax = jnp.einsum('bsd,edr->bser', x, lora_A)
        bax = jnp.einsum('bser,ero->bseo', ax, lora_B)
        logits = jnp.einsum('bsd,ed->bse', x, router_w) + router_b
        kth = jax.lax.top_k(logits, TOP_K)[0][..., -1:]
        masked = jnp.where(logits < kth, NEG_INF, logits)
        expert_weights = jax.nn.softmax(masked, axis=-1)
        return result + SCALING * jnp.einsum('bse,bseo->bso', expert_weights, bax)
    h = _L0_tok_ref(x, L0_tok_W, L0_tok_b, L0_tok_ln_gamma, L0_tok_ln_beta)
    h = h + _L0_attn_ref(_layernorm(h, axis=-1), L0_attn_Wq, L0_attn_bq, L0_attn_Wv, L0_attn_bv, L0_attn_hyperplanes)
    h = h + _L0_ffn_ref(_layernorm(h, axis=-1), L0_ffn_base_w, L0_ffn_base_b, L0_ffn_lora_A, L0_ffn_lora_B, L0_ffn_router_w, L0_ffn_router_b)
    return h

_drawn_inputs = setup_inputs


def setup_inputs(seed=0):
    import zlib

    import numpy as np

    out = dict(_drawn_inputs(seed))
    spreads = {'L0_tok_ln_gamma': (1.0, 0.2),
     'L0_tok_ln_beta': (0.0, 0.1),
     'L0_ffn_base_b': (0.0, 0.1),
     'L0_ffn_router_b': (0.0, 0.602)}
    factors = {'L0_attn_bv': 3.087}
    for name, (base, spread) in spreads.items():
        noise = np.random.default_rng([zlib.crc32(name.encode()), seed]).standard_normal(out[name].shape)
        drawn = base * np.exp(spread * noise) if base else spread * noise
        out[name] = jnp.asarray(drawn.astype(out[name].dtype))
    for name, factor in factors.items():
        out[name] = (out[name] * factor).astype(out[name].dtype)
    return out
```

```python
import concourse.bass as bass
from concourse import mybir
from contextlib import ExitStack

FP32, BF16, FP16, INT32 = mybir.dt.float32, mybir.dt.bfloat16, mybir.dt.float16, mybir.dt.int32
ALU = mybir.AluOpType
ACT = mybir.ActivationFunctionType
AX = mybir.AxisListType

BATCH, SEQ, FRAME, HID = 2, 4096, 80, 256
HEADS, DH, BITS = 16, 16, 6
BUCKETS = 1 << BITS
EXPERTS, RANK = 8, 16
TOKENS = BATCH * SEQ
P = 128
GROUP = 512
SUB = GROUP // P
GROUPS = TOKENS // GROUP
FB = HID // P
TT = SEQ // P
HALF = 2048
CHUNK = 1024
BANK = 512
ALL_HEADS = BATCH * HEADS
STEPS = 2 * (SEQ // HALF) * TT
HEAD_STEPS = STEPS // 2

LN_EPS = 1e-5
LORA_SCALE = 2.0
QS = 4.0
SCORE = 1.0 / (QS * QS * HID ** 0.5)
FAR, NEAR = float(BUCKETS - 2), float(BUCKETS - 1)
SAFE = 1700.0
KEEP_5_BITS = -(1 << 19)

X_SLOTS, C_SLOTS, P_SLOTS = 3, 4, 4


class Steps:

    def __init__(self, eng, sem, base):
        self.eng, self.sem, self.base, self.n = eng, sem, base, 0

    def mark(self, ins):
        ins.then_inc(self.sem, 1)
        self.n += 1
        return self.n

    def wait(self, n):
        self.eng.wait_ge(self.sem, self.base + n)


def audio_tower(nc, x_t, w_tok, gamma, beta, wq_t, bq, wv_t, bv, hyper, hyper_b, base_w_t, base_b, lora_a, lora_b,
                router_t, router_b, eye, powers, head_ones, bucket_of, expert_rows, out, force_general=False):
    q_parts = nc.dram_tensor("q_parts", (2, HID, TOKENS), FP16).ap()
    v_rows = nc.dram_tensor("v_rows", (TOKENS, HID), FP32).ap()
    code_rows = nc.dram_tensor("code_rows", (HEADS, TOKENS), BF16).ap()
    norm_rows = nc.dram_tensor("norm_rows", (HEADS, TOKENS), FP32).ap()
    nu_rows = nc.dram_tensor("nu_rows", (HEADS, BATCH, SEQ), FP16).ap()

    with ExitStack() as ctx:
        def sb(name, shape, dt):
            return ctx.enter_context(nc.sbuf_tensor(name, shape, dt))

        def sem(name):
            return ctx.enter_context(nc.semaphore(name))

        wtok_sb = sb("wtok_sb", [FRAME + 1, HID], FP32)
        gamma_sb = sb("gamma_sb", [P, HID], FP32)
        beta_sb = sb("beta_sb", [P, HID], FP32)
        wq_sb = sb("wq_sb", [P, FB, HID], FP32)
        wv_sb = sb("wv_sb", [P, FB, HID], FP32)
        base_sb = sb("base_sb", [P, FB, HID], FP32)
        lora_a_sb = sb("lora_a_sb", [P, FB, EXPERTS * RANK], FP32)
        lora_b_sb = sb("lora_b_sb", [P, HID], FP32)
        router_sb = sb("router_sb", [P, FB, EXPERTS], FP32)
        bq_sb = sb("bq_sb", [P, FB], FP32)
        rows_sb = sb("rows_sb", [1, 2 * HID + EXPERTS + P], FP32)
        bv_row = rows_sb[0:1, 0:HID]
        base_b_row = rows_sb[0:1, HID:2 * HID]
        router_b_row = rows_sb[0:1, 2 * HID:2 * HID + EXPERTS]
        ones_row = rows_sb[0:1, 2 * HID + EXPERTS:]
        eye_sb = sb("eye_sb", [P, P], FP32)
        plane_sb = sb("plane_sb", [P, FB, HEADS * BITS], FP32)
        plane_b = sb("plane_b", [HEADS * BITS, 1], FP32)
        powers_sb = sb("powers_sb", [HEADS * BITS, HEADS], FP16)
        ones_h = sb("ones_h", [P, FB, HEADS], FP32)
        bucket_col = sb("bucket_col", [P, 1], FP32)
        expert_sb = sb("expert_sb", [EXPERTS, P], FP32)
        wait_carrier = sb("wait_carrier", [1, 1], FP32)
        neg_half = sb("neg_half", [P, SUB], FP32)

        hidden = sb("hidden", [P, TOKENS // P, HID], FP32)
        code_cols = sb("code_cols", [P, TOKENS // P, HEADS], FP32)

        k_op = [sb(f"k_op{i}", [P, SEQ], FP16) for i in range(2)]
        q_op = [sb(f"q_op{i}", [P, SEQ], FP16) for i in range(2)]
        codes = [sb(f"codes{i}", [P, SEQ], BF16) for i in range(2)]
        code_col = [sb(f"code_col{i}", [P, TT], FP32) for i in range(2)]
        v_op = [sb(f"v_op{i}", [P, TT, 32], FP32) for i in range(2)]
        nu_b = sb("nu_b", [P, SEQ], FP16)
        coeff = sb("coeff", [P, C_SLOTS, HALF], BF16)
        att_sb = sb("att_sb", [P, 2, BANK], FP32)
        att_tok = sb("att_tok", [P, 16, DH], FP32)
        inv_den = sb("inv_den", [P, 16], FP32)

        work = sb("work", [P, P_SLOTS, HALF], FP32)
        flat = work[:, :, :].rearrange("p a b -> p (a b)")

        def scratch(at, n, shape=None):
            v = flat[:, at:at + n]
            return v.rearrange("p (a b) -> p a b", b=shape) if shape else v

        def narrow(at, n, rows, dt):
            return coeff[0:rows, :, :].rearrange("p a b -> p (a b)")[:, at:at + n].bitcast(dt)

        x_in = narrow(0, 2 * GROUP, FRAME + 1, FP32)
        y = scratch(0, 1024, HID)
        x1 = scratch(2048, 1024, HID)
        x1t = scratch(3072, 1024, GROUP)
        q32 = scratch(4096, 1024, GROUP)
        sq = scratch(5120, 1024, GROUP)
        v_sb = scratch(6144, 1024, HID)
        q16 = [scratch(7168, 512).bitcast(FP16).rearrange("p (a b) -> p a b", b=GROUP),
               scratch(7680, 512).bitcast(FP16).rearrange("p (a b) -> p a b", b=GROUP)]
        norm_sb = narrow(1024, 2 * GROUP, HEADS, FP32)
        bits = narrow(2048, GROUP, HEADS * BITS, FP16)
        code_sb = narrow(2560, GROUP, HEADS, BF16)
        stats = sb("stats", [P, SUB, 6], FP32)
        mv = sb("mv", [P, SUB, 2], FP32)
        var_e = sb("var_e", [P, SUB], FP32)
        rstd = sb("rstd", [P, SUB], FP32)

        x2, x2t = y, scratch(1024, 1024, GROUP)
        wax = scratch(2048, 512)
        w_exp = scratch(2560, 512)
        out_sb = scratch(3072, 1024, HID)
        logit = sb("logit", [P, SUB, EXPERTS], FP32)
        ranked = sb("ranked", [P, SUB, 8], FP32)
        e_w = sb("e_w", [P, SUB, EXPERTS], FP32)
        e_mask = sb("e_mask", [P, SUB, EXPERTS], FP32)
        e_sum = sb("e_sum", [P, SUB], FP32)
        e_inv = sb("e_inv", [P, SUB], FP32)
        w_t = narrow(3072, 2 * GROUP, EXPERTS, FP32)

        norms = flat[0:ALL_HEADS, 0:SEQ]
        mids = flat[0:ALL_HEADS, SEQ:2 * SEQ]
        nu16 = coeff[0:ALL_HEADS, 0:2, :].rearrange("p a b -> p (a b)").bitcast(FP16)
        peak = sb("peak", [32, 32], FP32)
        peak_t = sb("peak_t", [32, 32], FP32)
        peak_all = sb("peak_all", [1, 1], FP32)
        flag = sb("flag", [1, 1], INT32)
        row_max4 = sb("row_max4", [P, 4], FP32)
        row_max = sb("row_max", [P, TT], FP32)
        nu_t = sb("nu_t", [TT, P], FP32)
        nu_t16 = sb("nu_t16", [TT, P], FP16)

        psum = ctx.enter_context(nc.psum_tensor("psum", [P, 8 * BANK], FP32))

        def banks(a, n, shape=None, rows=P):
            v = psum[0:rows, a * BANK:(a + n) * BANK]
            return v.rearrange("p (a b) -> p a b", b=shape) if shape else v

        hp, xtp, qp, vp = banks(0, 2, HID), banks(2, 2, GROUP), banks(4, 2, GROUP), banks(6, 2, HID)
        planes_p, norm_p = banks(0, 1, rows=HEADS * BITS), banks(1, 1, rows=HEADS)
        code_row_p, code_col_p = banks(2, 1, rows=HEADS), banks(3, 1)[:, 0:SUB * HEADS]
        x_slot = [banks(2 * i, 2) for i in range(X_SLOTS)]
        acc = [banks(6, 1), banks(7, 1)]
        x2tp, logit_p, w_tp = banks(0, 2, GROUP), banks(2, 1)[:, 0:SUB * EXPERTS], banks(3, 1, rows=EXPERTS)
        axt_p, w_exp_p, out_p = banks(4, 1), banks(5, 1), banks(6, 2, HID)

        weights_in = sem("weights_in")
        planes_in = sem("planes_in")
        consts_set = sem("consts_set")
        x_loaded = sem("x_loaded")
        tok_ready = sem("tok_ready")
        vec = sem("vec")
        var_ready = sem("var_ready")
        rstd_ready = sem("rstd_ready")
        y_ready = sem("y_ready")
        gained = sem("gained")
        affine_ready = sem("affine_ready")
        gelu_ready = sem("gelu_ready")
        x1_ready = sem("x1_ready")
        x1t_psum = sem("x1t_psum")
        x1t_ready = sem("x1t_ready")
        q_psum = sem("q_psum")
        v_psum = sem("v_psum")
        q32_ready = sem("q32_ready")
        sq_ready = sem("sq_ready")
        v_ready = sem("v_ready")
        q16_ready = sem("q16_ready")
        planes_psum = sem("planes_psum")
        norm_psum = sem("norm_psum")
        bits_ready = sem("bits_ready")
        codes_psum = sem("codes_psum")
        norm_ready = sem("norm_ready")
        codes_ready = sem("codes_ready")
        q_stored = sem("q_stored")
        v_stored = sem("v_stored")
        code_stored = sem("code_stored")
        norm_stored = sem("norm_stored")
        norms_in = sem("norms_in")
        peak_ready = sem("peak_ready")
        mids_ready = sem("mids_ready")
        nu_ready = sem("nu_ready")
        nu_stored = sem("nu_stored")
        flag_ready = sem("flag_ready")
        gen_in = sem("gen_in")
        gen_scores = sem("gen_scores")
        gen_maxed = sem("gen_maxed")
        gen_turned = sem("gen_turned")
        gen_nu = sem("gen_nu")
        gen_vec = sem("gen_vec")
        gen_rows = sem("gen_rows")
        gen_zero = sem("gen_zero")
        gen_stored = sem("gen_stored")
        head_in = [sem(f"head_in{i}") for i in range(2)]
        onehots = sem("onehots")
        shift_rows = sem("shift_rows")
        code_col_ready = sem("code_col_ready")
        coeff_ready = sem("coeff_ready")
        scores_ready = sem("scores_ready")
        scaled = sem("scaled")
        probs_ready = sem("probs_ready")
        probs_used = sem("probs_used")
        acc_copied = sem("acc_copied")
        acc_turned = sem("acc_turned")
        acc_free = sem("acc_free")
        att_steps = sem("att_steps")
        key_hots = sem("key_hots")
        f_x2 = sem("f_x2")
        f_x2t_psum = sem("f_x2t_psum")
        f_x2t = sem("f_x2t")
        f_logits = sem("f_logits")
        f_diff = sem("f_diff")
        f_exp = sem("f_exp")
        f_w = sem("f_w")
        f_wt_psum = sem("f_wt_psum")
        f_wt = sem("f_wt")
        f_wexp_psum = sem("f_wexp_psum")
        f_wexp = sem("f_wexp")
        f_wax = sem("f_wax")
        f_out_psum = sem("f_out_psum")
        f_out = sem("f_out")
        stored = sem("stored")

        WEIGHT_LOADS = 18
        HEAD_LOADS = 11
        block = ctx.enter_context(nc.Block())

        def lag(eng, s, value):
            if not (isinstance(value, int) and value <= 0):
                eng.wait_ge(s, value)

        def over_groups(eng, body):
            body(0)
            with eng.Fori(1, GROUPS) as g:
                body(g)

        @block.sync
        def _(sp):
            n = 0
            for dst, src in (
                (wtok_sb[:, :], w_tok),
                (gamma_sb[:, :], gamma.rearrange("(a n) -> a n", a=1).broadcast_to((P, HID))),
                (beta_sb[:, :], beta.rearrange("(a n) -> a n", a=1).broadcast_to((P, HID))),
                (wq_sb[:, :, :], wq_t.rearrange("(c p) n -> p c n", p=P)),
                (wv_sb[:, :, :], wv_t.rearrange("(c p) n -> p c n", p=P)),
                (base_sb[:, :, :], base_w_t.rearrange("(c p) n -> p c n", p=P)),
                (lora_a_sb[:, :, :], lora_a.rearrange("(c p) n -> p c n", p=P)),
                (lora_b_sb[:, :], lora_b),
                (router_sb[:, :, :], router_t.rearrange("(c p) n -> p c n", p=P)),
                (bq_sb[:, :], bq),
                (bv_row, bv.rearrange("(a n) -> a n", a=1)),
                (base_b_row, base_b.rearrange("(a n) -> a n", a=1)),
                (router_b_row, router_b.rearrange("(a n) -> a n", a=1)),
                (eye_sb[:, :], eye),
                (powers_sb[:, :], powers),
                (ones_h[:, :, :], head_ones),
                (bucket_col[:, :], bucket_of),
                (expert_sb[:, :], expert_rows),
            ):
                sp.dma_start(dst, src).then_inc(weights_in, 16)
                n += 1
            assert n == WEIGHT_LOADS
            sp.wait_ge(consts_set, 1)
            for h in range(HEADS):
                f, r = divmod(h * DH, P)
                sp.dma_start(plane_sb[r:r + DH, f, h * BITS:(h + 1) * BITS], hyper[0:DH, :]).then_inc(planes_in, 16)
                sp.dma_start(plane_b[h * BITS:(h + 1) * BITS, :], hyper_b).then_inc(planes_in, 16)

            sp.wait_ge(consts_set, 3)

            def group(g):
                lag(sp, tok_ready, g)
                sp.dma_start(x_in[0:FRAME, :], x_t[:, bass.ds(g * GROUP, GROUP)]).then_inc(x_loaded, 16)

                def leave(g):
                    sp.wait_ge(v_ready, g + 1)
                    sp.wait_ge(q16_ready, g + 1)
                    sp.wait_ge(norm_ready, g + 1)
                    sp.dma_start(v_rows[bass.ds(g * GROUP, GROUP), :].rearrange("(k p) c -> p k c", p=P), v_sb).then_inc(v_stored, 16)
                    for part in range(2):
                        sp.dma_start(q_parts[part, :, bass.ds(g * GROUP, GROUP)].rearrange("(f p) s -> p f s", p=P), q16[part]).then_inc(q_stored, 16)
                    sp.dma_start(norm_rows[:, bass.ds(g * GROUP, GROUP)], norm_sb[:, :]).then_inc(norm_stored, 16)
                    sp.wait_ge(codes_ready, g + 1)
                    sp.dma_start(code_rows[:, bass.ds(g * GROUP, GROUP)], code_sb[:, :]).then_inc(code_stored, 16)
                leave(g)
            over_groups(sp, group)

            sp.wait_ge(norm_stored, 16 * GROUPS)
            sp.wait_ge(v_stored, 16 * GROUPS)
            sp.wait_ge(q_stored, 32 * GROUPS)
            sp.wait_ge(code_stored, 16 * GROUPS)
            for b in range(BATCH):
                sp.dma_start(norms[b * HEADS:(b + 1) * HEADS, :], norm_rows[:, b * SEQ:(b + 1) * SEQ]).then_inc(norms_in, 16)

            def operand_rows(k_dst, q_dst, h16, off, s):
                for i in range(4):
                    for dst, part in ((k_dst, i // 2), (q_dst, i % 2)):
                        sp.dma_start(dst[DH * i:DH * (i + 1), :],
                                     q_parts[part, bass.ds(h16, DH), bass.ds(off, SEQ)]).then_inc(s, 16)

            sp.wait_ge(flag_ready, 1)
            wide = sp.value_load(flag[0:1, 0:1], min_val=0, max_val=1)
            with sp.If(wide < 1):
                sp.wait_ge(nu_ready, 1)
                for b in range(BATCH):
                    sp.dma_start(nu_rows[:, b, :], nu16[b * HEADS:(b + 1) * HEADS, :]).then_inc(nu_stored, 16)
                sp.wait_ge(nu_stored, 16 * BATCH)
            with sp.Else():
                with sp.Fori(0, BATCH) as b:
                    with sp.Fori(0, HEADS) as local:
                        h = b * HEADS + local
                        sp.wait_ge(gen_nu, h + 1)
                        operand_rows(k_op[0], q_op[0], local * DH, b * SEQ, gen_in)
                        sp.wait_ge(gen_nu, h + 2)
                        sp.dma_start(nu_rows[bass.ds(local, 1), bass.ds(b, 1), :].rearrange("a b (i p) -> (a b i) p", p=P), nu_t16[:, :]).then_inc(nu_stored, 16)

                sp.wait_ge(nu_stored, 16 * ALL_HEADS)

            def load_head(b, local, odd, first=False):
                h = b * HEADS + local
                s = head_in[odd]
                if not first:
                    sp.wait_ge(probs_used, (h - 1) * HEAD_STEPS + P_SLOTS)
                operand_rows(k_op[odd], q_op[odd], local * DH, b * SEQ, s)
                sp.dma_start(codes[odd][:, :], code_rows[bass.ds(local, 1), bass.ds(b * SEQ, SEQ)].broadcast_to((P, SEQ))).then_inc(s, 16)
                sp.dma_start(v_op[odd][:, :, 0:DH],
                             v_rows[bass.ds(b * SEQ, SEQ), bass.ds(local * DH, DH)].rearrange("(i p) d -> p i d", p=P)).then_inc(s, 16)
                lag(sp, shift_rows, h)
                sp.dma_start(nu_b[P // 2:P, :], nu_rows[bass.ds(local, 1), bass.ds(b, 1), :].rearrange("a b s -> (a b) s").broadcast_to((P // 2, SEQ))).then_inc(s, 16)

            load_head(0, 0, 0, first=True)
            load_head(0, 1, 1, first=True)
            with sp.Fori(1, HEADS // 2) as pair:
                for odd in range(2):
                    load_head(0, pair * 2 + odd, odd)
            with sp.Fori(0, HEADS // 2) as pair:
                for odd in range(2):
                    load_head(1, pair * 2 + odd, odd)

            def out_group(g):
                sp.wait_ge(f_out, g + 1)
                sp.dma_start(out[bass.ds(g * GROUP, GROUP), :].rearrange("(k p) c -> p k c", p=P), out_sb).then_inc(stored, 16)
            with sp.Fori(0, GROUPS) as g:
                out_group(g)
            sp.wait_ge(stored, 16 * GROUPS)

        @block.gpsimd
        def _(pool):
            pool.memset(plane_sb[:, :, :], 0.0).then_inc(consts_set, 1)
            pool.memset(neg_half[:, :], -0.5).then_inc(consts_set, 1)
            pool.memset(x_in[:, :], 1.0).then_inc(consts_set, 1)
            pool.memset(ones_row, 1.0).then_inc(consts_set, 1)
            pool.wait_ge(consts_set, 4)
            pool.wait_ge(weights_in, 16 * WEIGHT_LOADS)

            def inv_sqrt(n):
                pool.wait_ge(var_ready, n)
                pool.tensor_tensor(rstd[:, :], var_e[:, :], neg_half[:, :], ALU.pow).then_inc(rstd_ready, 1)

            def group(g):
                inv_sqrt(g * 2 + 1)
                pool.wait_ge(y_ready, g + 1)
                pool.tensor_tensor(y, y, gamma_sb[:, :].unsqueeze(1).broadcast_to((P, SUB, HID)), ALU.mult).then_inc(gained, 1)
                pool.wait_ge(gained, g + 1)
                pool.tensor_tensor(y, y, beta_sb[:, :].unsqueeze(1).broadcast_to((P, SUB, HID)), ALU.add).then_inc(affine_ready, 1)
                inv_sqrt(g * 2 + 2)
            over_groups(pool, group)

            with pool.Fori(0, BATCH) as b:
                with pool.Fori(0, HEADS // 2) as pair:
                    for odd in range(2):
                        h = b * HEADS + pair * 2 + odd
                        pool.wait_ge(onehots, h + 1)
                        pool.tensor_copy(code_col[odd][:, :], code_cols[:, bass.ds(b * TT, TT), bass.ds(pair * 2 + odd, 1)].rearrange("p i a -> p (i a)")).then_inc(code_col_ready, 1)
                        pool.wait_ge(code_col_ready, h + 1)
                        pool.tensor_tensor(q_op[odd][P // 2:P, :], q_op[odd][P // 2:P, :], nu_b[P // 2:P, :], ALU.mult).then_inc(shift_rows, 1)
                        pool.wait_ge(shift_rows, h + 1)

            with pool.Fori(0, GROUPS) as g:
                inv_sqrt(g + 2 * GROUPS + 1)

        @block.scalar
        def _(act):
            act.wait_ge(weights_in, 16 * WEIGHT_LOADS)

            def group(g):
                act.wait_ge(affine_ready, g + 1)
                act.activation(hidden[:, bass.ds(g * SUB, SUB), :], y, ACT.Gelu).then_inc(gelu_ready, 1)
                act.wait_ge(x1t_psum, g + 1)
                act.activation(x1t, xtp, ACT.Copy).then_inc(x1t_ready, 1)
                act.wait_ge(q_psum, g + 1)
                for f in range(FB):
                    act.activation(q32[:, f, :], qp[:, f, :], ACT.Identity, bias=bq_sb[:, f:f + 1]).then_inc(q32_ready, 1)
                act.wait_ge(q32_ready, g * FB + FB)
                act.activation(sq, q32, ACT.Square, scale=QS).then_inc(sq_ready, 1)
                act.wait_ge(v_psum, g + 1)
                lag(act, v_stored, g * 16)
                act.activation(v_sb, vp, ACT.Copy).then_inc(v_ready, 1)
            over_groups(act, group)

            act.wait_ge(peak_ready, 1)
            act.activation(mids, norms, ACT.Sqrt, scale=peak[:, 0:1]).then_inc(mids_ready, 1)

            def copy_acc(rounds, half):
                act.wait_ge(probs_used, rounds * TT + P_SLOTS + TT)
                act.wait_ge(acc_turned, rounds + 1)
                act.activation(att_sb[:, half, :], acc[half], ACT.Copy).then_inc(acc_copied, 1)

            with act.Fori(0, ALL_HEADS // 2) as pair:
                for n in range(STEPS):
                    act.wait_ge(scaled, pair * (2 * STEPS) + (X_SLOTS + 2 * n + 2))
                    act.activation(work[:, n % P_SLOTS, :], work[:, n % P_SLOTS, :], ACT.Exp, scale=SCORE).then_inc(probs_ready, 1)
                    if n % TT == 3 and n > TT:
                        copy_acc(pair * 4 + (n // TT - 1), (n // TT - 1) % 2)
                copy_acc(pair * 4 + 3, 1)

            with act.Fori(0, GROUPS) as g:
                act.wait_ge(f_x2t_psum, g + 1)
                act.activation(x2t, x2tp, ACT.Copy).then_inc(f_x2t, 1)
                act.wait_ge(f_diff, g + 1)
                act.activation(e_w[:, :, :], e_w[:, :, :], ACT.Exp).then_inc(f_exp, 1)
                act.wait_ge(f_wt_psum, g + 1)
                act.activation(w_t[:, :], w_tp, ACT.Copy).then_inc(f_wt, 1)
                act.wait_ge(f_wexp_psum, g + 1)
                act.activation(w_exp, w_exp_p, ACT.Copy).then_inc(f_wexp, 1)

        @block.tensor
        def _(pe):
            pe.wait_ge(weights_in, 16 * WEIGHT_LOADS)
            pe.wait_ge(consts_set, 4)
            pe.wait_ge(planes_in, 32 * HEADS)

            def group(g):
                pe.wait_ge(x_loaded, g * 16 + 16)
                lag(pe, norm_ready, g)
                for k in range(SUB):
                    mm = pe.matmul(hp[:, k, :], x_in[:, k * P:(k + 1) * P], wtok_sb[:, :], start=True, stop=True)
                mm.then_inc(tok_ready, 1)
                pe.wait_ge(x1_ready, g + 1)
                lag(pe, codes_ready, g)
                for k in range(SUB):
                    for f in range(FB):
                        mm = pe.transpose(xtp[:, f, k * P:(k + 1) * P], x1[:, k, f * P:(f + 1) * P], eye_sb[:, :])
                mm.then_inc(x1t_psum, 1)
                pe.wait_ge(x1t_ready, g + 1)
                lag(pe, q32_ready, g * FB)
                for f in range(FB):
                    for c in range(FB):
                        mm = pe.matmul(qp[:, f, :], wq_sb[:, c, f * P:(f + 1) * P], x1t[:, c, :], start=(c == 0), stop=(c == FB - 1))
                mm.then_inc(q_psum, 1)
                lag(pe, v_ready, g)
                for k in range(SUB):
                    for c in range(FB):
                        pe.matmul(vp[:, k, :], x1t[:, c, k * P:(k + 1) * P], wv_sb[:, c, :], start=(c == 0), stop=False)
                    mm = pe.matmul(vp[:, k, :], ones_row, bv_row, start=False, stop=True)
                mm.then_inc(v_psum, 1)
                pe.wait_ge(q32_ready, g * FB + FB)
                pe.wait_ge(y_ready, g + 1)
                for f in range(FB):
                    mm = pe.matmul(planes_p, plane_sb[:, f, :], q32[:, f, :], start=(f == 0), stop=(f == FB - 1))
                mm.then_inc(planes_psum, 1)
                pe.wait_ge(sq_ready, g + 1)
                for f in range(FB):
                    mm = pe.matmul(norm_p, ones_h[:, f, :], sq[:, f, :], start=(f == 0), stop=(f == FB - 1))
                mm.then_inc(norm_psum, 1)
                pe.wait_ge(bits_ready, g + 1)
                pe.matmul(code_row_p, powers_sb[:, :], bits[:, :], start=True, stop=True)
                for k in range(SUB):
                    mm = pe.matmul(code_col_p[:, k * HEADS:(k + 1) * HEADS], bits[:, k * P:(k + 1) * P], powers_sb[:, :], start=True, stop=True)
                mm.then_inc(codes_psum, 1)
            over_groups(pe, group)

            pe.wait_ge(flag_ready, 1)
            wide = pe.value_load(flag[0:1, 0:1], min_val=0, max_val=1)
            with pe.If(wide > 0):
                pe.wait_ge(gen_zero, 2)
                with pe.Fori(0, ALL_HEADS) as h:
                    with pe.Fori(0, TT) as i:
                        pe.wait_ge(gen_in, h * (8 * 16) + 8 * 16)
                        for c in range(4):
                            n = (h * TT + i) * 4 + c
                            pe.wait_ge(gen_maxed, n + 1)
                            for j in range(2):
                                mm = pe.matmul(x_slot[c % 2][:, j * BANK:(j + 1) * BANK], q_op[0][:, bass.ds(i * P, P)],
                                               k_op[0][:, c * CHUNK + j * BANK:c * CHUNK + (j + 1) * BANK], start=True, stop=True)
                            mm.then_inc(gen_scores, 1)
                    pe.wait_ge(gen_rows, h * TT + TT)
                    pe.transpose(psum[0:TT, 4 * BANK:4 * BANK + P], row_max[:, :], eye_sb[:, :]).then_inc(gen_turned, 1)

            def slot_before(m):
                return m - X_SLOTS if m >= X_SLOTS else max(k for k in range(2 * STEPS) if k % X_SLOTS == m) - 2 * STEPS

            def scores(pair, n):
                odd, half, t = n // HEAD_STEPS, n // TT % 2, n % TT
                for sub in range(2):
                    m = 2 * n + sub
                    pe.wait_ge(scaled, pair * (2 * STEPS) + (X_SLOTS + slot_before(m) + 1))
                    for j in range(2):
                        q0 = half * HALF + sub * CHUNK + j * BANK
                        mm = pe.matmul(x_slot[m % X_SLOTS][:, j * BANK:(j + 1) * BANK], k_op[odd][:, t * P:(t + 1) * P],
                                       q_op[odd][:, q0:q0 + BANK], start=True, stop=True)
                    mm.then_inc(scores_ready, 1)

            def values(pair, n):
                odd, half, t = n // HEAD_STEPS, n // TT % 2, n % TT
                if t == 0:
                    pe.wait_ge(acc_free, pair * 4 + (n // TT + 1))
                pe.wait_ge(probs_ready, pair * STEPS + (n + 1))
                for j in range(4):
                    mm = pe.matmul(acc[half][32 * j:32 * (j + 1), :], v_op[odd][:, t, :], work[:, n % P_SLOTS, j * BANK:(j + 1) * BANK],
                                   start=(t == 0), stop=(t == TT - 1), tile_position=(0, 32 * j))
                mm.then_inc(probs_used, 1)

            def turn(rounds, half):
                pe.wait_ge(acc_copied, rounds + 1)
                for i in range(4):
                    mm = pe.transpose(acc[half][:, i * P:(i + 1) * P], att_sb[:, half, i * P:(i + 1) * P], eye_sb[:, :])
                mm.then_inc(acc_turned, 1)

            pe.wait_ge(shift_rows, 1)
            for n in range(2):
                scores(0, n)
            with pe.Fori(0, ALL_HEADS // 2) as pair:
                for n in range(STEPS):
                    values(pair, n)
                    if n + 2 == HEAD_STEPS:
                        pe.wait_ge(shift_rows, pair * 2 + 2)
                    if n + 2 < STEPS:
                        scores(pair, n + 2)
                    if n % TT == 4 and n > TT:
                        turn(pair * 4 + (n // TT - 1), (n // TT - 1) % 2)
                with pe.If(pair < ALL_HEADS // 2 - 1):
                    pe.wait_ge(shift_rows, pair * 2 + 3)
                    scores(pair + 1, 0)
                turn(pair * 4 + 3, 1)
                with pe.If(pair < ALL_HEADS // 2 - 1):
                    scores(pair + 1, 1)

            with pe.Fori(0, GROUPS) as g:
                pe.wait_ge(f_x2, g + 1)
                for k in range(SUB):
                    for f in range(FB):
                        mm = pe.transpose(x2tp[:, f, k * P:(k + 1) * P], x2[:, k, f * P:(f + 1) * P], eye_sb[:, :])
                mm.then_inc(f_x2t_psum, 1)
                pe.wait_ge(f_x2t, g + 1)
                for k in range(SUB):
                    for c in range(FB):
                        pe.matmul(logit_p[:, k * EXPERTS:(k + 1) * EXPERTS], x2t[:, c, k * P:(k + 1) * P], router_sb[:, c, :], start=(c == 0), stop=False)
                    mm = pe.matmul(logit_p[:, k * EXPERTS:(k + 1) * EXPERTS], ones_row, router_b_row, start=False, stop=True)
                mm.then_inc(f_logits, 1)
                for c in range(FB):
                    pe.matmul(axt_p, lora_a_sb[:, c, :], x2t[:, c, :], start=(c == 0), stop=(c == FB - 1))
                pe.wait_ge(f_w, g + 1)
                for k in range(SUB):
                    mm = pe.transpose(w_tp[:, k * P:(k + 1) * P], e_w[:, k, :], eye_sb[:, :])
                mm.then_inc(f_wt_psum, 1)
                pe.wait_ge(f_wt, g + 1)
                pe.matmul(w_exp_p, expert_sb[:, :], w_t[:, :], start=True, stop=True).then_inc(f_wexp_psum, 1)
                pe.wait_ge(f_wax, g + 1)
                for k in range(SUB):
                    for c in range(FB):
                        pe.matmul(out_p[:, k, :], x2t[:, c, k * P:(k + 1) * P], base_sb[:, c, :], start=(c == 0), stop=False)
                    pe.matmul(out_p[:, k, :], ones_row, base_b_row, start=False, stop=False)
                    mm = pe.matmul(out_p[:, k, :], wax[:, k * P:(k + 1) * P], lora_b_sb[:, :], start=False, stop=True)
                mm.then_inc(f_out_psum, 1)

        @block.vector
        def _(dve):
            PRO, EPI = 28, 23

            def apart(s):
                s.mark(dve.memset(wait_carrier[:, :], 0.0))

            def norm_stats(s, src, eps):
                apart(s)
                for k in range(SUB):
                    at = s.mark(dve.bn_stats(stats[:, k, :], src(k)))
                s.wait(at)
                apart(s)
                for k in range(SUB):
                    at = s.mark(dve.bn_aggr(mv[:, k, :], stats[:, k, :]))
                s.wait(at)
                dve.tensor_scalar(var_e[:, :], mv[:, :, 1], eps, None, ALU.add).then_inc(var_ready, 1)

            def normalise(s, dst, src, done):
                for k in range(SUB):
                    ins = dve.tensor_scalar(dst(k), src(k), mv[:, k, 0:1], rstd[:, k:k + 1], ALU.subtract, ALU.mult)
                    if k < SUB - 1:
                        s.mark(ins)
                ins.then_inc(done, 1)

            for i in range(2):
                dve.memset(v_op[i][:, :, :], 0.0).then_inc(vec, 1)
            dve.memset(peak[:, :], 0.0).then_inc(vec, 1)
            dve.wait_ge(vec, 3)
            for i in range(2):
                dve.memset(v_op[i][:, :, DH:DH + 1], 1.0).then_inc(vec, 1)
            dve.wait_ge(vec, 5)
            dve.wait_ge(planes_in, 32 * HEADS)
            dve.wait_ge(weights_in, 16 * WEIGHT_LOADS)
            VEC0 = 5

            def group(g):
                s = Steps(dve, vec, g * PRO + VEC0)
                dve.wait_ge(tok_ready, g + 1)
                norm_stats(s, lambda k: hp[:, k, :], LN_EPS)
                dve.wait_ge(rstd_ready, g * 2 + 1)
                normalise(s, lambda k: y[:, k, :], lambda k: hp[:, k, :], y_ready)
                dve.wait_ge(gelu_ready, g + 1)
                norm_stats(s, lambda k: hidden[:, bass.ds(g * SUB + k, 1), :].rearrange("p a c -> p (a c)"), LN_EPS)
                dve.wait_ge(rstd_ready, g * 2 + 2)
                normalise(s, lambda k: x1[:, k, :], lambda k: hidden[:, bass.ds(g * SUB + k, 1), :].rearrange("p a c -> p (a c)"), x1_ready)
                dve.wait_ge(q32_ready, g * FB + FB)
                lag(dve, q_stored, g * 32)
                s.wait(s.mark(dve.tensor_scalar(q16[0], q32, QS, None, ALU.mult)))
                dve.scalar_tensor_tensor(q16[1], q32, QS, q16[0], ALU.mult, ALU.subtract).then_inc(q16_ready, 1)
                dve.wait_ge(planes_psum, g + 1)
                dve.tensor_scalar(bits[:, :], planes_p, plane_b[:, 0:1], 0.0, ALU.add, ALU.is_ge).then_inc(bits_ready, 1)
                dve.wait_ge(norm_psum, g + 1)
                lag(dve, norm_stored, g * 16)
                dve.tensor_copy(norm_sb[:, :], norm_p).then_inc(norm_ready, 1)
                dve.wait_ge(codes_psum, g + 1)
                lag(dve, code_stored, g * 16)
                s.mark(dve.tensor_copy(code_sb[:, :], code_row_p))
                dve.tensor_copy(code_cols[:, bass.ds(g * SUB, SUB), :], code_col_p.rearrange("p (k h) -> p k h", h=HEADS)).then_inc(codes_ready, 1)
                assert s.n == PRO
            over_groups(dve, group)

            VEC1 = VEC0 + PRO * GROUPS
            s = Steps(dve, vec, VEC1)
            dve.wait_ge(norms_in, 16 * BATCH)
            dve.tensor_reduce(peak[:, 0:1], norms, AX.X, ALU.max).then_inc(peak_ready, 1)
            dve.wait_ge(peak_ready, 1)
            s.wait(s.mark(dve.transpose(peak_t[:, :], peak[:, :])))
            s.wait(s.mark(dve.tensor_reduce(peak_all[:, :], peak_t[0:1, :], AX.X, ALU.max)))
            s.wait(s.mark(dve.tensor_scalar(peak_all[:, :], peak_all[:, :], -1.0 if force_general else SAFE, None, ALU.is_le)))
            dve.tensor_scalar(flag[:, :], peak_all[:, :], -1.0, 1.0, ALU.mult, ALU.add).then_inc(flag_ready, 1)
            dve.wait_ge(mids_ready, 1)
            s.wait(s.mark(dve.tensor_tensor(mids, mids, norms, ALU.add)))
            s.wait(s.mark(dve.tensor_scalar(mids, mids, 0.5 / NEAR, None, ALU.mult)))
            s.wait(s.mark(dve.tensor_single_scalar(mids.bitcast(INT32), mids.bitcast(INT32), KEEP_5_BITS, ALU.bitwise_and)))
            dve.tensor_copy(nu16, mids).then_inc(nu_ready, 1)
            dve.wait_ge(nu_ready, 1)
            VEC2 = VEC1 + s.n

            wide = dve.value_load(flag[0:1, 0:1], min_val=0, max_val=1)
            with dve.If(wide > 0):
                dve.memset(x_slot[0], 0.0).then_inc(gen_maxed, 1)
                dve.memset(x_slot[1], 0.0).then_inc(gen_maxed, 1)
                dve.memset(q_op[0][P // 2:P, :], 0.0).then_inc(gen_zero, 1)
                dve.memset(k_op[0][P // 2:P, :], 0.0).then_inc(gen_zero, 1)
                dve.memset(nu_t16[:, :], 0.0).then_inc(gen_nu, 1)
                with dve.Fori(0, ALL_HEADS) as h:
                    with dve.Fori(0, TT) as i:
                        for c in range(4):
                            n = (h * TT + i) * 4 + c
                            dve.wait_ge(gen_scores, n + 1)
                            dve.tensor_reduce(row_max4[:, c:c + 1], x_slot[c % 2], AX.X, ALU.max).then_inc(gen_maxed, 1)
                        dve.wait_ge(gen_maxed, (h * TT + i) * 4 + 6)
                        dve.tensor_reduce(row_max[:, bass.ds(i, 1)], row_max4[:, :], AX.X, ALU.max).then_inc(gen_rows, 1)
                        dve.wait_ge(gen_rows, h * TT + i + 1)
                    dve.wait_ge(gen_turned, h + 1)
                    g2 = Steps(dve, gen_vec, h * 2)
                    g2.wait(g2.mark(dve.tensor_scalar(nu_t[:, :], psum[0:TT, 4 * BANK:4 * BANK + P], 1.0625 / FAR, None, ALU.mult)))
                    g2.wait(g2.mark(dve.tensor_single_scalar(nu_t[:, :].bitcast(INT32), nu_t[:, :].bitcast(INT32), KEEP_5_BITS, ALU.bitwise_and)))
                    dve.tensor_copy(nu_t16[:, :], nu_t[:, :]).then_inc(gen_nu, 1)
                    dve.wait_ge(nu_stored, h * 16 + 16)
            with dve.Else():
                dve.wait_ge(nu_stored, 16 * BATCH)

            for i in range(X_SLOTS):
                dve.memset(x_slot[i], 0.0).then_inc(scaled, 1)
            for i in range(P_SLOTS):
                dve.memset(work[:, i, :], 0.0).then_inc(probs_used, 1)
            for i in range(2):
                dve.memset(acc[i], 0.0).then_inc(acc_free, 1)
                dve.memset(att_sb[:, i, :], 0.0).then_inc(acc_turned, 1)
            dve.wait_ge(scaled, X_SLOTS)
            dve.wait_ge(acc_turned, 2)

            def onehot(nth, odd):
                dve.wait_ge(head_in[odd], nth * (16 * HEAD_LOADS) + 16 * HEAD_LOADS)
                up = slice(P // 2, P)
                dve.tensor_scalar(k_op[odd][up, :], codes[odd][up, :], bucket_col[up, 0:1], None, ALU.is_equal).then_inc(key_hots, 1)
                dve.tensor_scalar(q_op[odd][up, :], codes[odd][up, :], bucket_col[up, 0:1], NEAR, ALU.is_equal, ALU.subtract).then_inc(onehots, 1)

            def coefficient(pair, n):
                odd, half, t = n // HEAD_STEPS, n // TT % 2, n % TT
                if t == 0 and half == 0:
                    dve.wait_ge(code_col_ready, pair * 2 + (odd + 1))
                dve.tensor_scalar(coeff[:, n % C_SLOTS, :], codes[odd][:, half * HALF:(half + 1) * HALF], code_col[odd][:, t:t + 1],
                                  FAR, ALU.is_equal, ALU.add).then_inc(coeff_ready, 1)

            def attended(rounds, half, b, local):
                turned = acc[half].rearrange("p (i j d) -> p j i d", j=4, d=32)
                inv = inv_den[:, :].rearrange("p (j i) -> p j i", j=4)
                dve.wait_ge(acc_turned, rounds + 3)
                dve.reciprocal(inv, turned[:, :, :, DH]).then_inc(att_steps, 1)
                dve.wait_ge(att_steps, rounds * 2 + 1)
                dve.tensor_tensor(att_tok[:, :, :].rearrange("p (j i) d -> p j i d", j=4), turned[:, :, :, 0:DH],
                                  inv.unsqueeze(3).broadcast_to((P, 4, 4, DH)), ALU.mult).then_inc(acc_free, 1)
                dve.wait_ge(acc_free, rounds + 3)
                rows = hidden[:, bass.ds(b * TT + half * 16, 16), bass.ds(local * DH, DH)]
                dve.tensor_tensor(rows, rows, att_tok[:, :, :], ALU.add).then_inc(att_steps, 1)

            onehot(0, 0)

            def head_pair(pair, b, local):
                coefficient(pair, 0)
                for n in range(STEPS):
                    if n + 1 < STEPS:
                        coefficient(pair, n + 1)
                    for sub in range(2):
                        m = 2 * n + sub
                        dve.wait_ge(scores_ready, pair * (2 * STEPS) + (m + 1))
                        if sub == 0:
                            dve.wait_ge(probs_used, pair * STEPS + (n + 1))
                            dve.wait_ge(coeff_ready, pair * STEPS + (n + 1))
                        dve.tensor_tensor(work[:, n % P_SLOTS, sub * CHUNK:(sub + 1) * CHUNK], x_slot[m % X_SLOTS],
                                          coeff[:, n % C_SLOTS, sub * CHUNK:(sub + 1) * CHUNK], ALU.mult).then_inc(scaled, 1)
                    if n == 16:
                        onehot(pair, 1)
                    if n == HEAD_STEPS + 16:
                        with dve.If(pair < ALL_HEADS // 2 - 1):
                            onehot(pair + 1, 0)
                    if n % TT == 6 and n > TT:
                        r = n // TT - 1
                        attended(pair * 4 + r, r % 2, b, local + r // 2)
                attended(pair * 4 + 3, 1, b, local + 1)

            with dve.Fori(0, BATCH) as b:
                with dve.Fori(0, HEADS // 2) as p:
                    head_pair(b * (HEADS // 2) + p, b, p * 2)

            def after(g):
                s = Steps(dve, vec, g * EPI + VEC2)
                rows = lambda k: hidden[:, bass.ds(g * SUB + k, 1), :].rearrange("p a c -> p (a c)")
                norm_stats(s, rows, LN_EPS)
                dve.wait_ge(rstd_ready, g + 2 * GROUPS + 1)
                normalise(s, lambda k: x2[:, k, :], rows, f_x2)
                dve.wait_ge(f_logits, g + 1)
                s.wait(s.mark(dve.tensor_copy(logit[:, :, :], logit_p.rearrange("p (k e) -> p k e", e=EXPERTS))))
                apart(s)
                for k in range(SUB):
                    at = s.mark(dve.max(ranked[:, k, :], logit[:, k, :]))
                s.wait(at)
                dve.tensor_tensor(e_w[:, :, :], logit[:, :, :], ranked[:, :, 0:1].broadcast_to((P, SUB, EXPERTS)), ALU.subtract).then_inc(f_diff, 1)
                at = s.mark(dve.tensor_tensor(e_mask[:, :, :], logit[:, :, :], ranked[:, :, 1:2].broadcast_to((P, SUB, EXPERTS)), ALU.is_ge))
                dve.wait_ge(f_exp, g + 1)
                s.wait(at)
                s.wait(s.mark(dve.tensor_tensor(e_mask[:, :, :], e_w[:, :, :], e_mask[:, :, :], ALU.mult)))
                s.wait(s.mark(dve.tensor_reduce(e_sum[:, :], e_mask[:, :, :], AX.X, ALU.add)))
                s.wait(s.mark(dve.reciprocal(e_inv[:, :], e_sum[:, :])))
                dve.scalar_tensor_tensor(e_w[:, :, :], e_mask[:, :, :], LORA_SCALE, e_inv[:, :].unsqueeze(2).broadcast_to((P, SUB, EXPERTS)), ALU.mult, ALU.mult).then_inc(f_w, 1)
                dve.wait_ge(f_wexp, g + 1)
                dve.tensor_tensor(wax, axt_p, w_exp, ALU.mult).then_inc(f_wax, 1)
                dve.wait_ge(f_out_psum, g + 1)
                lag(dve, stored, g * 16)
                dve.tensor_tensor(out_sb, out_p, hidden[:, bass.ds(g * SUB, SUB), :], ALU.add).then_inc(f_out, 1)
                assert s.n == EPI
            over_groups(dve, after)


def kernel(**inputs):
    import numpy as _np
    import concourse.bacc as _bacc
    from concourse import mybir as _mybir
    from concourse.bass_utils import run_bass_kernel_spmd as _run

    x = inputs["x"]
    lay = _np.ascontiguousarray
    head_ones = _np.zeros((P, FB, HEADS), _np.float32)
    for h in range(HEADS):
        f, r = divmod(h * DH, P)
        head_ones[r:r + DH, f, h] = 1.0
    powers = _np.kron(_np.eye(HEADS), 2.0 ** _np.arange(BITS)[:, None]).astype(_np.float16)
    arrays = {
        "x_t": lay(_np.reshape(x, (TOKENS, FRAME)).T),
        "w_tok": lay(_np.concatenate([_np.asarray(inputs["L0_tok_W"]).T, _np.asarray(inputs["L0_tok_b"])[None]])),
        "gamma": inputs["L0_tok_ln_gamma"],
        "beta": inputs["L0_tok_ln_beta"],
        "wq_t": lay(_np.asarray(inputs["L0_attn_Wq"]).T),
        "bq": _np.reshape(inputs["L0_attn_bq"], (FB, P)).T,
        "wv_t": lay(_np.asarray(inputs["L0_attn_Wv"]).T),
        "bv": inputs["L0_attn_bv"],
        "hyper": inputs["L0_attn_hyperplanes"],
        "hyper_b": _np.asarray(inputs["L0_attn_hyperplanes"])[DH:].T,
        "base_w_t": lay(_np.asarray(inputs["L0_ffn_base_w"]).T),
        "base_b": inputs["L0_ffn_base_b"],
        "lora_a": lay(_np.reshape(_np.transpose(inputs["L0_ffn_lora_A"], (1, 0, 2)), (HID, EXPERTS * RANK))),
        "lora_b": lay(_np.reshape(inputs["L0_ffn_lora_B"], (EXPERTS * RANK, HID))),
        "router_t": lay(_np.asarray(inputs["L0_ffn_router_w"]).T),
        "router_b": inputs["L0_ffn_router_b"],
        "eye": _np.eye(P, dtype=_np.float32),
        "powers": powers,
        "head_ones": head_ones,
        "bucket_of": (_np.arange(P) % BUCKETS).astype(_np.float32)[:, None],
        "expert_rows": _np.kron(_np.eye(EXPERTS), _np.ones((1, RANK))).astype(_np.float32),
    }
    arrays = {k: lay(v) for k, v in arrays.items()}
    nc = _bacc.Bacc("TRN2", target_bir_lowering=False, num_devices=1)
    args = [nc.dram_tensor(k, v.shape, _mybir.dt.from_np(v.dtype), kind="ExternalInput").ap() for k, v in arrays.items()]
    out = nc.dram_tensor("out", (TOKENS, HID), FP32, kind="ExternalOutput").ap()
    audio_tower(nc, *args, out)
    r = _run(nc, [arrays], core_ids=[0])
    return _np.reshape(r.results[0]["out"], (BATCH, SEQ, HID))
```

```python
import concourse.bass as bass
from concourse import mybir
from contextlib import ExitStack

FP32, BF16, FP16, INT32 = mybir.dt.float32, mybir.dt.bfloat16, mybir.dt.float16, mybir.dt.int32
ALU = mybir.AluOpType
ACT = mybir.ActivationFunctionType
AX = mybir.AxisListType

BATCH, SEQ, FRAME, HID = 2, 4096, 80, 256
HEADS, DH, BITS = 16, 16, 6
BUCKETS = 1 << BITS
EXPERTS, RANK = 8, 16
TOKENS = BATCH * SEQ
P = 128
GROUP = 512
SUB = GROUP // P
GROUPS = TOKENS // GROUP
FB = HID // P
TT = SEQ // P
HALF = 2048
CHUNK = 1024
MULT = 1536
EXPD = HALF - MULT
BANK = 512
ALL_HEADS = BATCH * HEADS
STEPS = 2 * (SEQ // HALF) * TT
HEAD_STEPS = STEPS // 2

LN_EPS = 1e-5
LORA_SCALE = 2.0
QS = 4.0
SCORE = 1.0 / (QS * QS * HID ** 0.5)
FAR, NEAR = float(BUCKETS - 2), float(BUCKETS - 1)
SAFE = 1700.0
KEEP_5_BITS = -(1 << 19)

BIG = 30720.0

C_SLOTS, P_SLOTS, N_SLOTS = 3, 4, 2


class Steps:

    def __init__(self, eng, sem, base):
        self.eng, self.sem, self.base, self.n = eng, sem, base, 0

    def mark(self, ins):
        ins.then_inc(self.sem, 1)
        self.n += 1
        return self.n

    def wait(self, n):
        self.eng.wait_ge(self.sem, self.base + n)


def audio_tower(nc, x_t, w_tok, gamma, beta, wq_t, bq, wv_t, bv, hyper, hyper_b, base_w_t, base_b, lora_a, lora_b,
                router_t, router_b, eye, powers, head_ones, bucket_of, expert_rows, out, force_general=False):
    q_parts = nc.dram_tensor("q_parts", (2, HID, TOKENS), FP16).ap()
    v_rows = nc.dram_tensor("v_rows", (TOKENS, HID), FP32).ap()
    code_rows = nc.dram_tensor("code_rows", (HEADS, TOKENS), BF16).ap()
    norm_rows = nc.dram_tensor("norm_rows", (HEADS, TOKENS), FP32).ap()
    nu_rows = nc.dram_tensor("nu_rows", (HEADS, BATCH, SEQ), FP16).ap()

    with ExitStack() as ctx:
        def sb(name, shape, dt):
            return ctx.enter_context(nc.sbuf_tensor(name, shape, dt))

        def sem(name):
            return ctx.enter_context(nc.semaphore(name))

        wtok_sb = sb("wtok_sb", [FRAME + 1, HID], FP32)
        gamma_sb = sb("gamma_sb", [P, HID], FP32)
        beta_sb = sb("beta_sb", [P, HID], FP32)
        wq_sb = sb("wq_sb", [P, FB, HID], FP32)
        wv_sb = sb("wv_sb", [P, FB, HID], FP32)
        base_sb = sb("base_sb", [P, FB, HID], FP32)
        lora_a_sb = sb("lora_a_sb", [P, FB, EXPERTS * RANK], FP32)
        lora_b_sb = sb("lora_b_sb", [P, HID], FP32)
        router_sb = sb("router_sb", [P, FB, EXPERTS], FP32)
        bq_sb = sb("bq_sb", [P, FB], FP32)
        rows_sb = sb("rows_sb", [1, 2 * HID + EXPERTS + P], FP32)
        bv_row = rows_sb[0:1, 0:HID]
        base_b_row = rows_sb[0:1, HID:2 * HID]
        router_b_row = rows_sb[0:1, 2 * HID:2 * HID + EXPERTS]
        ones_row = rows_sb[0:1, 2 * HID + EXPERTS:]
        eye_sb = sb("eye_sb", [P, P], FP32)
        plane_sb = sb("plane_sb", [P, FB, HEADS * BITS], FP32)
        plane_b = sb("plane_b", [HEADS * BITS, 1], FP32)
        powers_sb = sb("powers_sb", [HEADS * BITS, HEADS], FP16)
        ones_h = sb("ones_h", [P, FB, HEADS], FP32)
        bucket_col = sb("bucket_col", [P, 1], FP32)
        expert_sb = sb("expert_sb", [EXPERTS, P], FP32)
        wait_carrier = sb("wait_carrier", [1, 1], FP32)
        neg_half = sb("neg_half", [P, SUB], FP32)

        hidden = sb("hidden", [P, TOKENS // P, HID], FP32)
        code_cols = sb("code_cols", [P, TOKENS // P, HEADS], FP32)

        k_op = [sb(f"k_op{i}", [P, SEQ], FP16) for i in range(2)]
        q_op = [sb(f"q_op{i}", [P, SEQ], FP16) for i in range(2)]
        codes = [sb(f"codes{i}", [P, SEQ], BF16) for i in range(2)]
        code_col = [sb(f"code_col{i}", [P, TT], FP32) for i in range(2)]
        v_op = [sb(f"v_op{i}", [P, TT, 32], FP32) for i in range(2)]
        nu_b = sb("nu_b", [P, SEQ], FP16)
        coeff = sb("coeff", [P, C_SLOTS, MULT], BF16)
        q_near = [sb(f"q_near{i}", [P, 2, EXPD], FP16) for i in range(2)]
        far_add = sb("far_add", [P, 2, EXPD], FP16)
        near_p = sb("near_p", [P, N_SLOTS, EXPD], FP32)
        att_sb = sb("att_sb", [P, 2, BANK], FP32)
        att_tok = sb("att_tok", [P, 16, DH], FP32)
        inv_den = sb("inv_den", [P, 16], FP32)

        work = sb("work", [P, P_SLOTS, HALF], FP32)
        flat = work[:, :, :].rearrange("p a b -> p (a b)")

        def scratch(at, n, shape=None):
            v = flat[:, at:at + n]
            return v.rearrange("p (a b) -> p a b", b=shape) if shape else v

        def narrow(at, n, rows, dt):
            return coeff[0:rows, :, :].rearrange("p a b -> p (a b)")[:, at:at + n].bitcast(dt)

        x_in = narrow(0, 2 * GROUP, FRAME + 1, FP32)
        y = scratch(0, 1024, HID)
        x1 = scratch(2048, 1024, HID)
        x1t = scratch(3072, 1024, GROUP)
        q32 = scratch(4096, 1024, GROUP)
        sq = scratch(5120, 1024, GROUP)
        v_sb = scratch(6144, 1024, HID)
        q16 = [scratch(7168, 512).bitcast(FP16).rearrange("p (a b) -> p a b", b=GROUP),
               scratch(7680, 512).bitcast(FP16).rearrange("p (a b) -> p a b", b=GROUP)]
        norm_sb = narrow(1024, 2 * GROUP, HEADS, FP32)
        bits = narrow(2048, GROUP, HEADS * BITS, FP16)
        code_sb = narrow(2560, GROUP, HEADS, BF16)
        stats = sb("stats", [P, SUB, 6], FP32)
        mv = sb("mv", [P, SUB, 2], FP32)
        var_e = sb("var_e", [P, SUB], FP32)
        rstd = sb("rstd", [P, SUB], FP32)

        x2, x2t = y, scratch(1024, 1024, GROUP)
        wax = scratch(2048, 512)
        w_exp = scratch(2560, 512)
        out_sb = scratch(3072, 1024, HID)
        logit = sb("logit", [P, SUB, EXPERTS], FP32)
        ranked = sb("ranked", [P, SUB, 8], FP32)
        e_w = sb("e_w", [P, SUB, EXPERTS], FP32)
        e_mask = sb("e_mask", [P, SUB, EXPERTS], FP32)
        e_sum = sb("e_sum", [P, SUB], FP32)
        e_inv = sb("e_inv", [P, SUB], FP32)
        w_t = narrow(3072, 2 * GROUP, EXPERTS, FP32)

        norms = flat[0:ALL_HEADS, 0:SEQ]
        mids = flat[0:ALL_HEADS, SEQ:2 * SEQ]
        nu16 = narrow(0, SEQ, ALL_HEADS, FP16)
        peak = sb("peak", [32, 32], FP32)
        peak_t = sb("peak_t", [32, 32], FP32)
        peak_all = sb("peak_all", [1, 1], FP32)
        flag = sb("flag", [1, 1], INT32)
        row_max4 = sb("row_max4", [P, 4], FP32)
        row_max = sb("row_max", [P, TT], FP32)
        nu_t = sb("nu_t", [TT, P], FP32)
        nu_t16 = sb("nu_t16", [TT, P], FP16)

        psum = ctx.enter_context(nc.psum_tensor("psum", [P, 8 * BANK], FP32))

        def banks(a, n, shape=None, rows=P):
            v = psum[0:rows, a * BANK:(a + n) * BANK]
            return v.rearrange("p (a b) -> p a b", b=shape) if shape else v

        hp, xtp, qp, vp = banks(0, 2, HID), banks(2, 2, GROUP), banks(4, 2, GROUP), banks(6, 2, HID)
        planes_p, norm_p = banks(0, 1, rows=HEADS * BITS), banks(1, 1, rows=HEADS)
        code_row_p, code_col_p = banks(2, 1, rows=HEADS), banks(3, 1)[:, 0:SUB * HEADS]
        x_slot = [banks(0, 2), banks(2, 2)]
        x_pair, x_single = banks(0, 2), [banks(2, 1), banks(3, 1)]
        x_far, x_near = banks(4, 1), banks(5, 1)
        acc = [banks(6, 1), banks(7, 1)]
        x2tp, logit_p, w_tp = banks(0, 2, GROUP), banks(2, 1)[:, 0:SUB * EXPERTS], banks(3, 1, rows=EXPERTS)
        axt_p, w_exp_p, out_p = banks(4, 1), banks(5, 1), banks(6, 2, HID)

        weights_in = sem("weights_in")
        planes_in = sem("planes_in")
        consts_set = sem("consts_set")
        x_loaded = sem("x_loaded")
        tok_ready = sem("tok_ready")
        vec = sem("vec")
        var_ready = sem("var_ready")
        rstd_ready = sem("rstd_ready")
        y_ready = sem("y_ready")
        gained = sem("gained")
        affine_ready = sem("affine_ready")
        gelu_ready = sem("gelu_ready")
        x1_ready = sem("x1_ready")
        x1t_psum = sem("x1t_psum")
        x1t_ready = sem("x1t_ready")
        q_psum = sem("q_psum")
        v_psum = sem("v_psum")
        q32_ready = sem("q32_ready")
        sq_ready = sem("sq_ready")
        v_ready = sem("v_ready")
        q16_ready = sem("q16_ready")
        planes_psum = sem("planes_psum")
        norm_psum = sem("norm_psum")
        bits_ready = sem("bits_ready")
        codes_psum = sem("codes_psum")
        norm_ready = sem("norm_ready")
        codes_ready = sem("codes_ready")
        q_stored = sem("q_stored")
        v_stored = sem("v_stored")
        code_stored = sem("code_stored")
        norm_stored = sem("norm_stored")
        norms_in = sem("norms_in")
        peak_ready = sem("peak_ready")
        mids_ready = sem("mids_ready")
        nu_ready = sem("nu_ready")
        nu_stored = sem("nu_stored")
        flag_ready = sem("flag_ready")
        gen_in = sem("gen_in")
        gen_scores = sem("gen_scores")
        gen_maxed = sem("gen_maxed")
        gen_turned = sem("gen_turned")
        gen_nu = sem("gen_nu")
        gen_vec = sem("gen_vec")
        gen_rows = sem("gen_rows")
        gen_zero = sem("gen_zero")
        gen_stored = sem("gen_stored")
        head_in = [sem(f"head_in{i}") for i in range(2)]
        onehots = sem("onehots")
        shift_rows = sem("shift_rows")
        code_col_ready = sem("code_col_ready")
        coeff_ready = sem("coeff_ready")
        pair_ready = sem("pair_ready")
        single_ready = sem("single_ready")
        masked_ready = sem("masked_ready")
        scaled = sem("scaled")
        masked_exp = sem("masked_exp")
        mixed = sem("mixed")
        probs_ready = sem("probs_ready")
        probs_used = sem("probs_used")
        acc_copied = sem("acc_copied")
        acc_turned = sem("acc_turned")
        acc_free = sem("acc_free")
        att_steps = sem("att_steps")
        key_hots = sem("key_hots")
        f_x2 = sem("f_x2")
        f_x2t_psum = sem("f_x2t_psum")
        f_x2t = sem("f_x2t")
        f_logits = sem("f_logits")
        f_diff = sem("f_diff")
        f_exp = sem("f_exp")
        f_w = sem("f_w")
        f_wt_psum = sem("f_wt_psum")
        f_wt = sem("f_wt")
        f_wexp_psum = sem("f_wexp_psum")
        f_wexp = sem("f_wexp")
        f_wax = sem("f_wax")
        f_out_psum = sem("f_out_psum")
        f_out = sem("f_out")
        stored = sem("stored")

        WEIGHT_LOADS = 18
        HEAD_LOADS = 15
        PIECE = 512
        PIECES = SEQ // PIECE + 4
        block = ctx.enter_context(nc.Block())

        def lag(eng, s, value):
            if not (isinstance(value, int) and value <= 0):
                eng.wait_ge(s, value)

        def over_groups(eng, body):
            body(0)
            with eng.Fori(1, GROUPS) as g:
                body(g)

        @block.sync
        def _(sp):
            n = 0
            for dst, src in (
                (wtok_sb[:, :], w_tok),
                (gamma_sb[:, :], gamma.rearrange("(a n) -> a n", a=1).broadcast_to((P, HID))),
                (beta_sb[:, :], beta.rearrange("(a n) -> a n", a=1).broadcast_to((P, HID))),
                (wq_sb[:, :, :], wq_t.rearrange("(c p) n -> p c n", p=P)),
                (wv_sb[:, :, :], wv_t.rearrange("(c p) n -> p c n", p=P)),
                (base_sb[:, :, :], base_w_t.rearrange("(c p) n -> p c n", p=P)),
                (lora_a_sb[:, :, :], lora_a.rearrange("(c p) n -> p c n", p=P)),
                (lora_b_sb[:, :], lora_b),
                (router_sb[:, :, :], router_t.rearrange("(c p) n -> p c n", p=P)),
                (bq_sb[:, :], bq),
                (bv_row, bv.rearrange("(a n) -> a n", a=1)),
                (base_b_row, base_b.rearrange("(a n) -> a n", a=1)),
                (router_b_row, router_b.rearrange("(a n) -> a n", a=1)),
                (eye_sb[:, :], eye),
                (powers_sb[:, :], powers),
                (ones_h[:, :, :], head_ones),
                (bucket_col[:, :], bucket_of),
                (expert_sb[:, :], expert_rows),
            ):
                sp.dma_start(dst, src).then_inc(weights_in, 16)
                n += 1
            assert n == WEIGHT_LOADS
            sp.wait_ge(consts_set, 1)
            for h in range(HEADS):
                f, r = divmod(h * DH, P)
                sp.dma_start(plane_sb[r:r + DH, f, h * BITS:(h + 1) * BITS], hyper[0:DH, :]).then_inc(planes_in, 16)
                sp.dma_start(plane_b[h * BITS:(h + 1) * BITS, :], hyper_b).then_inc(planes_in, 16)

            sp.wait_ge(consts_set, 3)

            def group(g):
                lag(sp, tok_ready, g)
                sp.dma_start(x_in[0:FRAME, :], x_t[:, bass.ds(g * GROUP, GROUP)]).then_inc(x_loaded, 16)

                def leave(g):
                    sp.wait_ge(v_ready, g + 1)
                    sp.wait_ge(q16_ready, g + 1)
                    sp.wait_ge(norm_ready, g + 1)
                    sp.dma_start(v_rows[bass.ds(g * GROUP, GROUP), :].rearrange("(k p) c -> p k c", p=P), v_sb).then_inc(v_stored, 16)
                    for part in range(2):
                        sp.dma_start(q_parts[part, :, bass.ds(g * GROUP, GROUP)].rearrange("(f p) s -> p f s", p=P), q16[part]).then_inc(q_stored, 16)
                    sp.dma_start(norm_rows[:, bass.ds(g * GROUP, GROUP)], norm_sb[:, :]).then_inc(norm_stored, 16)
                    sp.wait_ge(codes_ready, g + 1)
                    sp.dma_start(code_rows[:, bass.ds(g * GROUP, GROUP)], code_sb[:, :]).then_inc(code_stored, 16)
                leave(g)
            over_groups(sp, group)

            sp.wait_ge(norm_stored, 16 * GROUPS)
            sp.wait_ge(v_stored, 16 * GROUPS)
            sp.wait_ge(q_stored, 32 * GROUPS)
            sp.wait_ge(code_stored, 16 * GROUPS)
            for b in range(BATCH):
                sp.dma_start(norms[b * HEADS:(b + 1) * HEADS, :], norm_rows[:, b * SEQ:(b + 1) * SEQ]).then_inc(norms_in, 16)

            def operand_rows(k_dst, q_dst, h16, off, s):
                for i in range(4):
                    for dst, part in ((k_dst, i // 2), (q_dst, i % 2)):
                        sp.dma_start(dst[DH * i:DH * (i + 1), :],
                                     q_parts[part, bass.ds(h16, DH), bass.ds(off, SEQ)]).then_inc(s, 16)

            sp.wait_ge(flag_ready, 1)
            wide = sp.value_load(flag[0:1, 0:1], min_val=0, max_val=1)
            with sp.If(wide < 1):
                sp.wait_ge(nu_ready, 1)
                for b in range(BATCH):
                    sp.dma_start(nu_rows[:, b, :], nu16[b * HEADS:(b + 1) * HEADS, :]).then_inc(nu_stored, 16)
                sp.wait_ge(nu_stored, 16 * BATCH)
            with sp.Else():
                with sp.Fori(0, BATCH) as b:
                    with sp.Fori(0, HEADS) as local:
                        h = b * HEADS + local
                        sp.wait_ge(gen_nu, h + 1)
                        operand_rows(k_op[0], q_op[0], local * DH, b * SEQ, gen_in)
                        sp.wait_ge(gen_nu, h + 2)
                        sp.dma_start(nu_rows[bass.ds(local, 1), bass.ds(b, 1), :].rearrange("a b (i p) -> (a b i) p", p=P), nu_t16[:, :]).then_inc(nu_stored, 16)

                sp.wait_ge(nu_stored, 16 * ALL_HEADS)

            def load_head(b, local, odd, first=False):
                h = b * HEADS + local
                s = head_in[odd]
                if not first:
                    sp.wait_ge(probs_used, (h - 1) * HEAD_STEPS + P_SLOTS)
                operand_rows(k_op[odd], q_op[odd], local * DH, b * SEQ, s)
                for i in range(4):
                    sp.dma_start(q_near[odd][DH * i:DH * (i + 1), :, :],
                                 q_parts[i % 2, bass.ds(local * DH, DH), bass.ds(b * SEQ, SEQ)].rearrange("d (a s) -> d a s", a=2)[:, :, MULT:HALF]).then_inc(s, 16)
                sp.dma_start(codes[odd][:, :], code_rows[bass.ds(local, 1), bass.ds(b * SEQ, SEQ)].broadcast_to((P, SEQ))).then_inc(s, 16)
                sp.dma_start(v_op[odd][:, :, 0:DH],
                             v_rows[bass.ds(b * SEQ, SEQ), bass.ds(local * DH, DH)].rearrange("(i p) d -> p i d", p=P)).then_inc(s, 16)
                lag(sp, shift_rows, h * PIECES)
                sp.dma_start(nu_b[P // 2:P, :], nu_rows[bass.ds(local, 1), bass.ds(b, 1), :].rearrange("a b s -> (a b) s").broadcast_to((P // 2, SEQ))).then_inc(s, 16)

            load_head(0, 0, 0, first=True)
            load_head(0, 1, 1, first=True)
            with sp.Fori(1, HEADS // 2) as pair:
                for odd in range(2):
                    load_head(0, pair * 2 + odd, odd)
            with sp.Fori(0, HEADS // 2) as pair:
                for odd in range(2):
                    load_head(1, pair * 2 + odd, odd)

            def out_group(g):
                sp.wait_ge(f_out, g + 1)
                sp.dma_start(out[bass.ds(g * GROUP, GROUP), :].rearrange("(k p) c -> p k c", p=P), out_sb).then_inc(stored, 16)
            with sp.Fori(0, GROUPS) as g:
                out_group(g)
            sp.wait_ge(stored, 16 * GROUPS)

        @block.gpsimd
        def _(pool):
            pool.memset(plane_sb[:, :, :], 0.0).then_inc(consts_set, 1)
            pool.memset(neg_half[:, :], -0.5).then_inc(consts_set, 1)
            pool.memset(x_in[:, :], 1.0).then_inc(consts_set, 1)
            pool.memset(ones_row, 1.0).then_inc(consts_set, 1)
            pool.wait_ge(consts_set, 4)
            pool.wait_ge(weights_in, 16 * WEIGHT_LOADS)

            def inv_sqrt(n):
                pool.wait_ge(var_ready, n)
                pool.tensor_tensor(rstd[:, :], var_e[:, :], neg_half[:, :], ALU.pow).then_inc(rstd_ready, 1)

            def group(g):
                inv_sqrt(g * 2 + 1)
                pool.wait_ge(y_ready, g + 1)
                pool.tensor_tensor(y, y, gamma_sb[:, :].unsqueeze(1).broadcast_to((P, SUB, HID)), ALU.mult).then_inc(gained, 1)
                pool.wait_ge(gained, g + 1)
                pool.tensor_tensor(y, y, beta_sb[:, :].unsqueeze(1).broadcast_to((P, SUB, HID)), ALU.add).then_inc(affine_ready, 1)
                inv_sqrt(g * 2 + 2)
            over_groups(pool, group)

            up = slice(P // 2, P)

            def piece(h, odd, i):
                if i < SEQ // PIECE:
                    to = q_op[odd][up, i * PIECE:(i + 1) * PIECE]
                    pool.tensor_tensor(to, to, nu_b[up, i * PIECE:(i + 1) * PIECE], ALU.mult).then_inc(shift_rows, 1)
                else:
                    c, far = divmod(i - SEQ // PIECE, 2)
                    std = q_op[odd][up, c * HALF + MULT:(c + 1) * HALF]
                    if far:
                        pool.tensor_tensor(std, std, far_add[up, c, :], ALU.add).then_inc(shift_rows, 1)
                    else:
                        pool.tensor_tensor(q_near[odd][up, c, :], q_near[odd][up, c, :], std, ALU.add).then_inc(shift_rows, 1)
                pool.wait_ge(shift_rows, h * PIECES + (i + 1))

            pool.wait_ge(onehots, 1)
            for i in range(PIECES):
                piece(0, 0, i)
            with pool.Fori(0, BATCH) as b:
                with pool.Fori(0, HEADS // 2) as p:
                    pair = b * (HEADS // 2) + p
                    for n in range(STEPS):
                        pool.wait_ge(masked_exp, pair * (2 * STEPS) + (2 * n + 4))
                        to = work[:, n % P_SLOTS, MULT:HALF]
                        pool.tensor_tensor(to, to, near_p[:, n % N_SLOTS, :], ALU.add).then_inc(mixed, 1)
                        if 20 <= n < 20 + PIECES:
                            pool.wait_ge(mixed, pair * STEPS + (n + N_SLOTS + 1))
                            if n == 20:
                                pool.wait_ge(onehots, pair * 2 + 2)
                            piece(pair * 2 + 1, 1, n - 20)
                        if HEAD_STEPS + 20 <= n < HEAD_STEPS + 20 + PIECES:
                            with pool.If(pair < ALL_HEADS // 2 - 1):
                                pool.wait_ge(mixed, pair * STEPS + (n + N_SLOTS + 1))
                                if n == HEAD_STEPS + 20:
                                    pool.wait_ge(onehots, pair * 2 + 3)
                                piece(pair * 2 + 2, 0, n - HEAD_STEPS - 20)

            with pool.Fori(0, GROUPS) as g:
                inv_sqrt(g + 2 * GROUPS + 1)

        @block.scalar
        def _(act):
            act.wait_ge(weights_in, 16 * WEIGHT_LOADS)

            def group(g):
                act.wait_ge(affine_ready, g + 1)
                act.activation(hidden[:, bass.ds(g * SUB, SUB), :], y, ACT.Gelu).then_inc(gelu_ready, 1)
                act.wait_ge(x1t_psum, g + 1)
                act.activation(x1t, xtp, ACT.Copy).then_inc(x1t_ready, 1)
                act.wait_ge(q_psum, g + 1)
                for f in range(FB):
                    act.activation(q32[:, f, :], qp[:, f, :], ACT.Identity, bias=bq_sb[:, f:f + 1]).then_inc(q32_ready, 1)
                act.wait_ge(q32_ready, g * FB + FB)
                act.activation(sq, q32, ACT.Square, scale=QS).then_inc(sq_ready, 1)
                act.wait_ge(v_psum, g + 1)
                lag(act, v_stored, g * 16)
                act.activation(v_sb, vp, ACT.Copy).then_inc(v_ready, 1)
            over_groups(act, group)

            act.wait_ge(peak_ready, 1)
            act.activation(mids, norms, ACT.Sqrt, scale=peak[:, 0:1]).then_inc(mids_ready, 1)

            def copy_acc(rounds, half):
                act.wait_ge(probs_used, rounds * TT + P_SLOTS + TT)
                act.wait_ge(acc_turned, rounds + 1)
                act.activation(att_sb[:, half, :], acc[half], ACT.Copy).then_inc(acc_copied, 1)

            with act.Fori(0, ALL_HEADS // 2) as pair:
                for n in range(STEPS):
                    act.wait_ge(probs_used, pair * STEPS + (n + 1))
                    act.wait_ge(mixed, pair * STEPS + (n + 1))
                    act.wait_ge(masked_ready, pair * STEPS + (n + 1))
                    act.activation(work[:, n % P_SLOTS, MULT:HALF], x_far, ACT.Exp, scale=FAR * SCORE).then_inc(masked_exp, 1)
                    act.activation(near_p[:, n % N_SLOTS, :], x_near, ACT.Exp, scale=NEAR * SCORE).then_inc(masked_exp, 1)
                    act.wait_ge(scaled, pair * (2 * STEPS) + (2 * n + 5))
                    act.activation(work[:, n % P_SLOTS, 0:MULT], work[:, n % P_SLOTS, 0:MULT], ACT.Exp, scale=SCORE).then_inc(probs_ready, 1)
                    if n % TT == 3 and n > TT:
                        copy_acc(pair * 4 + (n // TT - 1), (n // TT - 1) % 2)
                copy_acc(pair * 4 + 3, 1)

            with act.Fori(0, GROUPS) as g:
                act.wait_ge(f_x2t_psum, g + 1)
                act.activation(x2t, x2tp, ACT.Copy).then_inc(f_x2t, 1)
                act.wait_ge(f_diff, g + 1)
                act.activation(e_w[:, :, :], e_w[:, :, :], ACT.Exp).then_inc(f_exp, 1)
                act.wait_ge(f_wt_psum, g + 1)
                act.activation(w_t[:, :], w_tp, ACT.Copy).then_inc(f_wt, 1)
                act.wait_ge(f_wexp_psum, g + 1)
                act.activation(w_exp, w_exp_p, ACT.Copy).then_inc(f_wexp, 1)

        @block.tensor
        def _(pe):
            pe.wait_ge(weights_in, 16 * WEIGHT_LOADS)
            pe.wait_ge(consts_set, 4)
            pe.wait_ge(planes_in, 32 * HEADS)

            def group(g):
                pe.wait_ge(x_loaded, g * 16 + 16)
                lag(pe, norm_ready, g)
                for k in range(SUB):
                    mm = pe.matmul(hp[:, k, :], x_in[:, k * P:(k + 1) * P], wtok_sb[:, :], start=True, stop=True)
                mm.then_inc(tok_ready, 1)
                pe.wait_ge(x1_ready, g + 1)
                lag(pe, codes_ready, g)
                for k in range(SUB):
                    for f in range(FB):
                        mm = pe.transpose(xtp[:, f, k * P:(k + 1) * P], x1[:, k, f * P:(f + 1) * P], eye_sb[:, :])
                mm.then_inc(x1t_psum, 1)
                pe.wait_ge(x1t_ready, g + 1)
                lag(pe, q32_ready, g * FB)
                for f in range(FB):
                    for c in range(FB):
                        mm = pe.matmul(qp[:, f, :], wq_sb[:, c, f * P:(f + 1) * P], x1t[:, c, :], start=(c == 0), stop=(c == FB - 1))
                mm.then_inc(q_psum, 1)
                lag(pe, v_ready, g)
                for k in range(SUB):
                    for c in range(FB):
                        pe.matmul(vp[:, k, :], x1t[:, c, k * P:(k + 1) * P], wv_sb[:, c, :], start=(c == 0), stop=False)
                    mm = pe.matmul(vp[:, k, :], ones_row, bv_row, start=False, stop=True)
                mm.then_inc(v_psum, 1)
                pe.wait_ge(q32_ready, g * FB + FB)
                pe.wait_ge(y_ready, g + 1)
                for f in range(FB):
                    mm = pe.matmul(planes_p, plane_sb[:, f, :], q32[:, f, :], start=(f == 0), stop=(f == FB - 1))
                mm.then_inc(planes_psum, 1)
                pe.wait_ge(sq_ready, g + 1)
                for f in range(FB):
                    mm = pe.matmul(norm_p, ones_h[:, f, :], sq[:, f, :], start=(f == 0), stop=(f == FB - 1))
                mm.then_inc(norm_psum, 1)
                pe.wait_ge(bits_ready, g + 1)
                pe.matmul(code_row_p, powers_sb[:, :], bits[:, :], start=True, stop=True)
                for k in range(SUB):
                    mm = pe.matmul(code_col_p[:, k * HEADS:(k + 1) * HEADS], bits[:, k * P:(k + 1) * P], powers_sb[:, :], start=True, stop=True)
                mm.then_inc(codes_psum, 1)
            over_groups(pe, group)

            pe.wait_ge(flag_ready, 1)
            wide = pe.value_load(flag[0:1, 0:1], min_val=0, max_val=1)
            with pe.If(wide > 0):
                pe.wait_ge(gen_zero, 2)
                with pe.Fori(0, ALL_HEADS) as h:
                    with pe.Fori(0, TT) as i:
                        pe.wait_ge(gen_in, h * (8 * 16) + 8 * 16)
                        for c in range(4):
                            n = (h * TT + i) * 4 + c
                            pe.wait_ge(gen_maxed, n + 1)
                            for j in range(2):
                                mm = pe.matmul(x_slot[c % 2][:, j * BANK:(j + 1) * BANK], q_op[0][:, bass.ds(i * P, P)],
                                               k_op[0][:, c * CHUNK + j * BANK:c * CHUNK + (j + 1) * BANK], start=True, stop=True)
                            mm.then_inc(gen_scores, 1)
                    pe.wait_ge(gen_rows, h * TT + TT)
                    pe.transpose(psum[0:TT, 4 * BANK:4 * BANK + P], row_max[:, :], eye_sb[:, :]).then_inc(gen_turned, 1)

            def scores(pair, n):
                odd, half, t = n // HEAD_STEPS, n // TT % 2, n % TT
                keys = k_op[odd][:, t * P:(t + 1) * P]
                pe.wait_ge(scaled, pair * (2 * STEPS) + (2 * n + 2))
                for j in range(2):
                    q0 = half * HALF + j * BANK
                    mm = pe.matmul(x_pair[:, j * BANK:(j + 1) * BANK], keys, q_op[odd][:, q0:q0 + BANK], start=True, stop=True)
                mm.then_inc(pair_ready, 1)
                q0 = half * HALF + CHUNK
                pe.matmul(x_single[n % 2], keys, q_op[odd][:, q0:q0 + BANK], start=True, stop=True).then_inc(single_ready, 1)

            def masked_scores(pair, n):
                odd, half, t = n // HEAD_STEPS, n // TT % 2, n % TT
                keys = k_op[odd][:, t * P:(t + 1) * P]
                pe.wait_ge(masked_exp, pair * (2 * STEPS) + (2 * n + 2))
                pe.matmul(x_far, keys, q_op[odd][:, half * HALF + MULT:(half + 1) * HALF], start=True, stop=True)
                pe.matmul(x_near, keys, q_near[odd][:, half, :], start=True, stop=True).then_inc(masked_ready, 1)

            def values(pair, n):
                odd, half, t = n // HEAD_STEPS, n // TT % 2, n % TT
                if t == 0:
                    pe.wait_ge(acc_free, pair * 4 + (n // TT + 1))
                pe.wait_ge(probs_ready, pair * STEPS + (n + 1))
                pe.wait_ge(mixed, pair * STEPS + (n + N_SLOTS + 1))
                for j in range(4):
                    mm = pe.matmul(acc[half][32 * j:32 * (j + 1), :], v_op[odd][:, t, :], work[:, n % P_SLOTS, j * BANK:(j + 1) * BANK],
                                   start=(t == 0), stop=(t == TT - 1), tile_position=(0, 32 * j))
                mm.then_inc(probs_used, 1)

            def turn(rounds, half):
                pe.wait_ge(acc_copied, rounds + 1)
                for i in range(4):
                    mm = pe.transpose(acc[half][:, i * P:(i + 1) * P], att_sb[:, half, i * P:(i + 1) * P], eye_sb[:, :])
                mm.then_inc(acc_turned, 1)

            pe.wait_ge(shift_rows, PIECES)
            for n in range(2):
                scores(0, n)
                masked_scores(0, n)
            with pe.Fori(0, ALL_HEADS // 2) as pair:
                for n in range(STEPS):
                    if n + 2 == HEAD_STEPS:
                        pe.wait_ge(shift_rows, pair * (2 * PIECES) + 2 * PIECES)
                    if n + 2 < STEPS:
                        scores(pair, n + 2)
                        values(pair, n)
                        masked_scores(pair, n + 2)
                    else:
                        if n + 2 == STEPS:
                            with pe.If(pair < ALL_HEADS // 2 - 1):
                                pe.wait_ge(shift_rows, pair * (2 * PIECES) + 3 * PIECES)
                                scores(pair + 1, 0)
                        values(pair, n)
                        with pe.If(pair < ALL_HEADS // 2 - 1):
                            if n + 1 == STEPS:
                                scores(pair + 1, 1)
                            masked_scores(pair + 1, n + 2 - STEPS)
                    if n % TT == 4 and n > TT:
                        turn(pair * 4 + (n // TT - 1), (n // TT - 1) % 2)
                turn(pair * 4 + 3, 1)

            with pe.Fori(0, GROUPS) as g:
                pe.wait_ge(f_x2, g + 1)
                for k in range(SUB):
                    for f in range(FB):
                        mm = pe.transpose(x2tp[:, f, k * P:(k + 1) * P], x2[:, k, f * P:(f + 1) * P], eye_sb[:, :])
                mm.then_inc(f_x2t_psum, 1)
                pe.wait_ge(f_x2t, g + 1)
                for k in range(SUB):
                    for c in range(FB):
                        pe.matmul(logit_p[:, k * EXPERTS:(k + 1) * EXPERTS], x2t[:, c, k * P:(k + 1) * P], router_sb[:, c, :], start=(c == 0), stop=False)
                    mm = pe.matmul(logit_p[:, k * EXPERTS:(k + 1) * EXPERTS], ones_row, router_b_row, start=False, stop=True)
                mm.then_inc(f_logits, 1)
                for c in range(FB):
                    pe.matmul(axt_p, lora_a_sb[:, c, :], x2t[:, c, :], start=(c == 0), stop=(c == FB - 1))
                pe.wait_ge(f_w, g + 1)
                for k in range(SUB):
                    mm = pe.transpose(w_tp[:, k * P:(k + 1) * P], e_w[:, k, :], eye_sb[:, :])
                mm.then_inc(f_wt_psum, 1)
                pe.wait_ge(f_wt, g + 1)
                pe.matmul(w_exp_p, expert_sb[:, :], w_t[:, :], start=True, stop=True).then_inc(f_wexp_psum, 1)
                pe.wait_ge(f_wax, g + 1)
                for k in range(SUB):
                    for c in range(FB):
                        pe.matmul(out_p[:, k, :], x2t[:, c, k * P:(k + 1) * P], base_sb[:, c, :], start=(c == 0), stop=False)
                    pe.matmul(out_p[:, k, :], ones_row, base_b_row, start=False, stop=False)
                    mm = pe.matmul(out_p[:, k, :], wax[:, k * P:(k + 1) * P], lora_b_sb[:, :], start=False, stop=True)
                mm.then_inc(f_out_psum, 1)

        @block.vector
        def _(dve):
            PRO, EPI = 28, 23

            def apart(s):
                s.mark(dve.memset(wait_carrier[:, :], 0.0))

            def norm_stats(s, src, eps):
                apart(s)
                for k in range(SUB):
                    at = s.mark(dve.bn_stats(stats[:, k, :], src(k)))
                s.wait(at)
                apart(s)
                for k in range(SUB):
                    at = s.mark(dve.bn_aggr(mv[:, k, :], stats[:, k, :]))
                s.wait(at)
                dve.tensor_scalar(var_e[:, :], mv[:, :, 1], eps, None, ALU.add).then_inc(var_ready, 1)

            def normalise(s, dst, src, done):
                for k in range(SUB):
                    ins = dve.tensor_scalar(dst(k), src(k), mv[:, k, 0:1], rstd[:, k:k + 1], ALU.subtract, ALU.mult)
                    if k < SUB - 1:
                        s.mark(ins)
                ins.then_inc(done, 1)

            for i in range(2):
                dve.memset(v_op[i][:, :, :], 0.0).then_inc(vec, 1)
            dve.memset(peak[:, :], 0.0).then_inc(vec, 1)
            dve.wait_ge(vec, 3)
            for i in range(2):
                dve.memset(v_op[i][:, :, DH:DH + 1], 1.0).then_inc(vec, 1)
            dve.wait_ge(vec, 5)
            dve.wait_ge(planes_in, 32 * HEADS)
            dve.wait_ge(weights_in, 16 * WEIGHT_LOADS)
            VEC0 = 5

            def group(g):
                s = Steps(dve, vec, g * PRO + VEC0)
                dve.wait_ge(tok_ready, g + 1)
                norm_stats(s, lambda k: hp[:, k, :], LN_EPS)
                dve.wait_ge(rstd_ready, g * 2 + 1)
                normalise(s, lambda k: y[:, k, :], lambda k: hp[:, k, :], y_ready)
                dve.wait_ge(gelu_ready, g + 1)
                norm_stats(s, lambda k: hidden[:, bass.ds(g * SUB + k, 1), :].rearrange("p a c -> p (a c)"), LN_EPS)
                dve.wait_ge(rstd_ready, g * 2 + 2)
                normalise(s, lambda k: x1[:, k, :], lambda k: hidden[:, bass.ds(g * SUB + k, 1), :].rearrange("p a c -> p (a c)"), x1_ready)
                dve.wait_ge(q32_ready, g * FB + FB)
                lag(dve, q_stored, g * 32)
                s.wait(s.mark(dve.tensor_scalar(q16[0], q32, QS, None, ALU.mult)))
                dve.scalar_tensor_tensor(q16[1], q32, QS, q16[0], ALU.mult, ALU.subtract).then_inc(q16_ready, 1)
                dve.wait_ge(planes_psum, g + 1)
                dve.tensor_scalar(bits[:, :], planes_p, plane_b[:, 0:1], 0.0, ALU.add, ALU.is_ge).then_inc(bits_ready, 1)
                dve.wait_ge(norm_psum, g + 1)
                lag(dve, norm_stored, g * 16)
                dve.tensor_copy(norm_sb[:, :], norm_p).then_inc(norm_ready, 1)
                dve.wait_ge(codes_psum, g + 1)
                lag(dve, code_stored, g * 16)
                s.mark(dve.tensor_copy(code_sb[:, :], code_row_p))
                dve.tensor_copy(code_cols[:, bass.ds(g * SUB, SUB), :], code_col_p.rearrange("p (k h) -> p k h", h=HEADS)).then_inc(codes_ready, 1)
                assert s.n == PRO
            over_groups(dve, group)

            VEC1 = VEC0 + PRO * GROUPS
            s = Steps(dve, vec, VEC1)
            dve.wait_ge(norms_in, 16 * BATCH)
            dve.tensor_reduce(peak[:, 0:1], norms, AX.X, ALU.max).then_inc(peak_ready, 1)
            dve.wait_ge(peak_ready, 1)
            s.wait(s.mark(dve.transpose(peak_t[:, :], peak[:, :])))
            s.wait(s.mark(dve.tensor_reduce(peak_all[:, :], peak_t[0:1, :], AX.X, ALU.max)))
            s.wait(s.mark(dve.tensor_scalar(peak_all[:, :], peak_all[:, :], -1.0 if force_general else SAFE, None, ALU.is_le)))
            dve.tensor_scalar(flag[:, :], peak_all[:, :], -1.0, 1.0, ALU.mult, ALU.add).then_inc(flag_ready, 1)
            dve.wait_ge(mids_ready, 1)
            s.wait(s.mark(dve.tensor_tensor(mids, mids, norms, ALU.add)))
            s.wait(s.mark(dve.tensor_scalar(mids, mids, 0.5 / NEAR, None, ALU.mult)))
            s.wait(s.mark(dve.tensor_single_scalar(mids.bitcast(INT32), mids.bitcast(INT32), KEEP_5_BITS, ALU.bitwise_and)))
            dve.tensor_copy(nu16, mids).then_inc(nu_ready, 1)
            dve.wait_ge(nu_ready, 1)
            VEC2 = VEC1 + s.n

            wide = dve.value_load(flag[0:1, 0:1], min_val=0, max_val=1)
            with dve.If(wide > 0):
                dve.memset(x_slot[0], 0.0).then_inc(gen_maxed, 1)
                dve.memset(x_slot[1], 0.0).then_inc(gen_maxed, 1)
                dve.memset(q_op[0][P // 2:P, :], 0.0).then_inc(gen_zero, 1)
                dve.memset(k_op[0][P // 2:P, :], 0.0).then_inc(gen_zero, 1)
                dve.memset(nu_t16[:, :], 0.0).then_inc(gen_nu, 1)
                with dve.Fori(0, ALL_HEADS) as h:
                    with dve.Fori(0, TT) as i:
                        for c in range(4):
                            n = (h * TT + i) * 4 + c
                            dve.wait_ge(gen_scores, n + 1)
                            dve.tensor_reduce(row_max4[:, c:c + 1], x_slot[c % 2], AX.X, ALU.max).then_inc(gen_maxed, 1)
                        dve.wait_ge(gen_maxed, (h * TT + i) * 4 + 6)
                        dve.tensor_reduce(row_max[:, bass.ds(i, 1)], row_max4[:, :], AX.X, ALU.max).then_inc(gen_rows, 1)
                        dve.wait_ge(gen_rows, h * TT + i + 1)
                    dve.wait_ge(gen_turned, h + 1)
                    g2 = Steps(dve, gen_vec, h * 2)
                    g2.wait(g2.mark(dve.tensor_scalar(nu_t[:, :], psum[0:TT, 4 * BANK:4 * BANK + P], 1.0625 / FAR, None, ALU.mult)))
                    g2.wait(g2.mark(dve.tensor_single_scalar(nu_t[:, :].bitcast(INT32), nu_t[:, :].bitcast(INT32), KEEP_5_BITS, ALU.bitwise_and)))
                    dve.tensor_copy(nu_t16[:, :], nu_t[:, :]).then_inc(gen_nu, 1)
                    dve.wait_ge(nu_stored, h * 16 + 16)
            with dve.Else():
                dve.wait_ge(nu_stored, 16 * BATCH)

            for bank in (x_pair, *x_single):
                dve.memset(bank, 0.0).then_inc(scaled, 1)
            for bank in (x_far, x_near):
                dve.memset(bank, 0.0).then_inc(masked_exp, 1)
            dve.memset(inv_den[:, :], 0.0).then_inc(att_steps, 1)
            dve.memset(att_tok[:, :, :], 0.0).then_inc(att_steps, 1)
            for i in range(N_SLOTS):
                dve.memset(near_p[:, i, :], 0.0).then_inc(mixed, 1)
            for i in range(P_SLOTS):
                dve.memset(work[:, i, :], 0.0).then_inc(probs_used, 1)
            for i in range(2):
                dve.memset(acc[i], 0.0).then_inc(acc_free, 1)
                dve.memset(att_sb[:, i, :], 0.0).then_inc(acc_turned, 1)

            def onehot(nth, odd, b, local):
                dve.wait_ge(head_in[odd], nth * (16 * HEAD_LOADS) + 16 * HEAD_LOADS)
                up = slice(P // 2, P)
                dve.tensor_scalar(k_op[odd][up, :], codes[odd][up, :], bucket_col[up, 0:1], None, ALU.is_equal).then_inc(key_hots, 1)
                last = codes[odd][up, :].rearrange("p (a s) -> p a s", a=2)[:, :, MULT:HALF]
                dve.tensor_scalar(q_near[odd][up, :, :], last, bucket_col[up, 0:1], -BIG, ALU.not_equal, ALU.mult).then_inc(key_hots, 1)
                dve.tensor_scalar(far_add[up, :, :], last, bucket_col[up, 0:1], -BIG, ALU.is_equal, ALU.mult).then_inc(key_hots, 1)
                dve.tensor_scalar(q_op[odd][up, :], codes[odd][up, :], bucket_col[up, 0:1], NEAR, ALU.is_equal, ALU.subtract).then_inc(onehots, 1)
                dve.tensor_copy(code_col[odd][:, :], code_cols[:, bass.ds(b * TT, TT), bass.ds(local, 1)].rearrange("p i a -> p (i a)")).then_inc(code_col_ready, 1)

            def coefficient(pair, n):
                odd, half, t = n // HEAD_STEPS, n // TT % 2, n % TT
                if t == 0 and half == 0:
                    dve.wait_ge(code_col_ready, pair * 2 + (odd + 1))
                dve.tensor_scalar(coeff[:, n % C_SLOTS, :], codes[odd][:, half * HALF:half * HALF + MULT], code_col[odd][:, t:t + 1],
                                  FAR, ALU.is_equal, ALU.add).then_inc(coeff_ready, 1)

            def attended(rounds, half, b, local):
                turned = acc[half].rearrange("p (i j d) -> p j i d", j=4, d=32)
                inv = inv_den[:, :].rearrange("p (j i) -> p j i", j=4)
                dve.wait_ge(acc_turned, rounds + 3)
                dve.reciprocal(inv, turned[:, :, :, DH]).then_inc(att_steps, 1)
                dve.wait_ge(att_steps, rounds * 2 + 3)
                dve.tensor_tensor(att_tok[:, :, :].rearrange("p (j i) d -> p j i d", j=4), turned[:, :, :, 0:DH],
                                  inv.unsqueeze(3).broadcast_to((P, 4, 4, DH)), ALU.mult).then_inc(acc_free, 1)
                dve.wait_ge(acc_free, rounds + 3)
                rows = hidden[:, bass.ds(b * TT + half * 16, 16), bass.ds(local * DH, DH)]
                dve.tensor_tensor(rows, rows, att_tok[:, :, :], ALU.add).then_inc(att_steps, 1)

            onehot(0, 0, 0, 0)

            def scale(pair, n, tile, q0, width):
                dve.tensor_tensor(work[:, n % P_SLOTS, q0:q0 + width], tile, coeff[:, n % C_SLOTS, q0:q0 + width], ALU.mult).then_inc(scaled, 1)

            def head_pair(pair, b, p):
                dve.wait_ge(scaled, pair * (2 * STEPS) + 3)
                coefficient(pair, 0)
                for n in range(STEPS):
                    if n + 1 < STEPS:
                        if n >= 2:
                            dve.wait_ge(scaled, pair * (2 * STEPS) + (2 * n + 1))
                        coefficient(pair, n + 1)
                    dve.wait_ge(probs_used, pair * STEPS + (n + 1))
                    dve.wait_ge(coeff_ready, pair * STEPS + (n + 1))
                    dve.wait_ge(pair_ready, pair * STEPS + (n + 1))
                    scale(pair, n, x_pair, 0, CHUNK)
                    dve.wait_ge(single_ready, pair * STEPS + (n + 1))
                    scale(pair, n, x_single[n % 2], CHUNK, BANK)
                    if n == 6:
                        with dve.If(p > 0):
                            attended(pair * 4 - 1, 1, b, (p * 2 + HEADS - 1) & (HEADS - 1))
                        with dve.Else():
                            with dve.If(b > 0):
                                attended(pair * 4 - 1, 1, 0, HEADS - 1)
                    if n == 12:
                        onehot(pair, 1, b, p * 2 + 1)
                    if n == HEAD_STEPS + 12:
                        with dve.If(p < HEADS // 2 - 1):
                            onehot(pair + 1, 0, b, (p * 2 + 2) & (HEADS - 1))
                        with dve.Else():
                            with dve.If(b < 1):
                                onehot(pair + 1, 0, 1, 0)
                    if n % TT == 6 and n > TT:
                        r = n // TT - 1
                        attended(pair * 4 + r, r % 2, b, p * 2 + r // 2)

            with dve.Fori(0, BATCH) as b:
                with dve.Fori(0, HEADS // 2) as p:
                    head_pair(b * (HEADS // 2) + p, b, p)
            attended(2 * ALL_HEADS - 1, 1, 1, HEADS - 1)

            def after(g):
                s = Steps(dve, vec, g * EPI + VEC2)
                rows = lambda k: hidden[:, bass.ds(g * SUB + k, 1), :].rearrange("p a c -> p (a c)")
                norm_stats(s, rows, LN_EPS)
                dve.wait_ge(rstd_ready, g + 2 * GROUPS + 1)
                normalise(s, lambda k: x2[:, k, :], rows, f_x2)
                dve.wait_ge(f_logits, g + 1)
                s.wait(s.mark(dve.tensor_copy(logit[:, :, :], logit_p.rearrange("p (k e) -> p k e", e=EXPERTS))))
                apart(s)
                for k in range(SUB):
                    at = s.mark(dve.max(ranked[:, k, :], logit[:, k, :]))
                s.wait(at)
                dve.tensor_tensor(e_w[:, :, :], logit[:, :, :], ranked[:, :, 0:1].broadcast_to((P, SUB, EXPERTS)), ALU.subtract).then_inc(f_diff, 1)
                at = s.mark(dve.tensor_tensor(e_mask[:, :, :], logit[:, :, :], ranked[:, :, 1:2].broadcast_to((P, SUB, EXPERTS)), ALU.is_ge))
                dve.wait_ge(f_exp, g + 1)
                s.wait(at)
                s.wait(s.mark(dve.tensor_tensor(e_mask[:, :, :], e_w[:, :, :], e_mask[:, :, :], ALU.mult)))
                s.wait(s.mark(dve.tensor_reduce(e_sum[:, :], e_mask[:, :, :], AX.X, ALU.add)))
                s.wait(s.mark(dve.reciprocal(e_inv[:, :], e_sum[:, :])))
                dve.scalar_tensor_tensor(e_w[:, :, :], e_mask[:, :, :], LORA_SCALE, e_inv[:, :].unsqueeze(2).broadcast_to((P, SUB, EXPERTS)), ALU.mult, ALU.mult).then_inc(f_w, 1)
                dve.wait_ge(f_wexp, g + 1)
                dve.tensor_tensor(wax, axt_p, w_exp, ALU.mult).then_inc(f_wax, 1)
                dve.wait_ge(f_out_psum, g + 1)
                lag(dve, stored, g * 16)
                dve.tensor_tensor(out_sb, out_p, hidden[:, bass.ds(g * SUB, SUB), :], ALU.add).then_inc(f_out, 1)
                assert s.n == EPI
            over_groups(dve, after)


def kernel(**inputs):
    import numpy as _np
    import concourse.bacc as _bacc
    from concourse import mybir as _mybir
    from concourse.bass_utils import run_bass_kernel_spmd as _run

    x = inputs["x"]
    lay = _np.ascontiguousarray
    head_ones = _np.zeros((P, FB, HEADS), _np.float32)
    for h in range(HEADS):
        f, r = divmod(h * DH, P)
        head_ones[r:r + DH, f, h] = 1.0
    powers = _np.kron(_np.eye(HEADS), 2.0 ** _np.arange(BITS)[:, None]).astype(_np.float16)
    arrays = {
        "x_t": lay(_np.reshape(x, (TOKENS, FRAME)).T),
        "w_tok": lay(_np.concatenate([_np.asarray(inputs["L0_tok_W"]).T, _np.asarray(inputs["L0_tok_b"])[None]])),
        "gamma": inputs["L0_tok_ln_gamma"],
        "beta": inputs["L0_tok_ln_beta"],
        "wq_t": lay(_np.asarray(inputs["L0_attn_Wq"]).T),
        "bq": _np.reshape(inputs["L0_attn_bq"], (FB, P)).T,
        "wv_t": lay(_np.asarray(inputs["L0_attn_Wv"]).T),
        "bv": inputs["L0_attn_bv"],
        "hyper": inputs["L0_attn_hyperplanes"],
        "hyper_b": _np.asarray(inputs["L0_attn_hyperplanes"])[DH:].T,
        "base_w_t": lay(_np.asarray(inputs["L0_ffn_base_w"]).T),
        "base_b": inputs["L0_ffn_base_b"],
        "lora_a": lay(_np.reshape(_np.transpose(inputs["L0_ffn_lora_A"], (1, 0, 2)), (HID, EXPERTS * RANK))),
        "lora_b": lay(_np.reshape(inputs["L0_ffn_lora_B"], (EXPERTS * RANK, HID))),
        "router_t": lay(_np.asarray(inputs["L0_ffn_router_w"]).T),
        "router_b": inputs["L0_ffn_router_b"],
        "eye": _np.eye(P, dtype=_np.float32),
        "powers": powers,
        "head_ones": head_ones,
        "bucket_of": (_np.arange(P) % BUCKETS).astype(_np.float32)[:, None],
        "expert_rows": _np.kron(_np.eye(EXPERTS), _np.ones((1, RANK))).astype(_np.float32),
    }
    arrays = {k: lay(v) for k, v in arrays.items()}
    nc = _bacc.Bacc("TRN2", target_bir_lowering=False, num_devices=1)
    args = [nc.dram_tensor(k, v.shape, _mybir.dt.from_np(v.dtype), kind="ExternalInput").ap() for k, v in arrays.items()]
    out = nc.dram_tensor("out", (TOKENS, HID), FP32, kind="ExternalOutput").ap()
    audio_tower(nc, *args, out)
    r = _run(nc, [arrays], core_ids=[0])
    return _np.reshape(r.results[0]["out"], (BATCH, SEQ, HID))
```

```python
import concourse.bass as bass
from concourse import mybir
from contextlib import ExitStack

FP32, BF16, FP16, INT32 = mybir.dt.float32, mybir.dt.bfloat16, mybir.dt.float16, mybir.dt.int32
ALU = mybir.AluOpType
ACT = mybir.ActivationFunctionType
AX = mybir.AxisListType

BATCH, SEQ, FRAME, HID = 2, 4096, 80, 256
HEADS, DH, BITS = 16, 16, 6
BUCKETS = 1 << BITS
EXPERTS, RANK = 8, 16
TOKENS = BATCH * SEQ
P = 128
GROUP = 512
SUB = GROUP // P
GROUPS = TOKENS // GROUP
FB = HID // P
TT = SEQ // P
HALF = 2048
CHUNK = 1024
MULT = 1536
EXPD = HALF - MULT
BANK = 512
ALL_HEADS = BATCH * HEADS
STEPS = 2 * (SEQ // HALF) * TT
HEAD_STEPS = STEPS // 2

LN_EPS = 1e-5
LORA_SCALE = 2.0
QS = 4.0
SCORE = 1.0 / (QS * QS * HID ** 0.5)
FAR, NEAR = float(BUCKETS - 2), float(BUCKETS - 1)
SAFE = 1700.0
KEEP_5_BITS = -(1 << 19)

BIG = 30720.0

C_SLOTS, P_SLOTS = 3, 4


class Steps:

    def __init__(self, eng, sem, base):
        self.eng, self.sem, self.base, self.n = eng, sem, base, 0

    def mark(self, ins):
        ins.then_inc(self.sem, 1)
        self.n += 1
        return self.n

    def wait(self, n):
        self.eng.wait_ge(self.sem, self.base + n)


def audio_tower(nc, x_t, w_tok, gamma, beta, wq_t, bq, wv_t, bv, hyper, hyper_b, base_w_t, base_b, lora_a, lora_b,
                router_t, router_b, eye, powers, head_ones, bucket_of, expert_rows, out, force_general=False):
    q_parts = nc.dram_tensor("q_parts", (2, HID, TOKENS), FP16).ap()
    q_near_parts = nc.dram_tensor("q_near_parts", (2, HID, TOKENS), FP16).ap()
    v_rows = nc.dram_tensor("v_rows", (TOKENS, HID), FP32).ap()
    code_rows = nc.dram_tensor("code_rows", (HEADS, TOKENS), BF16).ap()
    norm_rows = nc.dram_tensor("norm_rows", (HEADS, TOKENS), FP32).ap()
    nu_rows = nc.dram_tensor("nu_rows", (HEADS, BATCH, SEQ), FP16).ap()

    with ExitStack() as ctx:
        def sb(name, shape, dt):
            return ctx.enter_context(nc.sbuf_tensor(name, shape, dt))

        def sem(name):
            return ctx.enter_context(nc.semaphore(name))

        base_sb = sb("base_sb", [P, FB, HID], FP32)
        lora_a_sb = sb("lora_a_sb", [P, FB, EXPERTS * RANK], FP32)
        lora_b_sb = sb("lora_b_sb", [P, HID], FP32)
        router_sb = sb("router_sb", [P, FB, EXPERTS], FP32)
        bq_sb = sb("bq_sb", [P, FB], FP32)
        base_b_sb = sb("base_b_sb", [P, HID], FP32)
        rows_sb = sb("rows_sb", [1, EXPERTS + P], FP32)
        router_b_row = rows_sb[0:1, 0:EXPERTS]
        ones_row = rows_sb[0:1, EXPERTS:]
        eye_sb = sb("eye_sb", [P, P], FP32)
        plane_sb = sb("plane_sb", [P, FB, HEADS * BITS], FP32)
        plane_b = sb("plane_b", [HEADS * BITS, 1], FP32)
        powers_sb = sb("powers_sb", [HEADS * BITS, HEADS], FP16)
        ones_h = sb("ones_h", [P, FB, HEADS], BF16)
        bucket_col = sb("bucket_col", [P, 1], FP32)
        expert_sb = sb("expert_sb", [EXPERTS, P], FP32)
        wait_carrier = sb("wait_carrier", [1, 1], FP32)
        neg_half = sb("neg_half", [P, SUB], FP32)

        hidden = sb("hidden", [P, TOKENS // P, HID], FP32)
        code_cols = sb("code_cols", [P, TOKENS // P, HEADS], FP32)

        k_op = [sb(f"k_op{i}", [P, SEQ], FP16) for i in range(2)]
        q_op = [sb(f"q_op{i}", [P, SEQ], FP16) for i in range(2)]
        codes = [sb(f"codes{i}", [P, SEQ], BF16) for i in range(2)]
        code_col = [sb(f"code_col{i}", [P, TT], FP32) for i in range(2)]
        v_op = [sb(f"v_op{i}", [P, TT, 32], FP32) for i in range(2)]
        nu_b = sb("nu_b", [P, SEQ], FP16)
        neg_near = sb("neg_near", [P, 256], FP16)
        near_add = sb("near_add", [P, 2, EXPD], FP16)

        def early(at, n, rows=P):
            return q_op[1][0:rows, 2 * at:2 * (at + n)].bitcast(FP32)

        wq_sb = early(0, 512).rearrange("p (c n) -> p c n", c=FB)
        wv_sb = early(512, 512).rearrange("p (c n) -> p c n", c=FB)
        gamma_sb, beta_sb, wtok_sb = early(1024, 256), early(1280, 256), early(1536, 256, FRAME + 1)
        bv_sb = early(1792, 256)

        coeff = sb("coeff", [P, C_SLOTS, MULT], BF16)
        q_near = [sb(f"q_near{i}", [P, 2, EXPD], FP16) for i in range(2)]
        far_add = sb("far_add", [P, 2, EXPD], FP16)
        att_sb = sb("att_sb", [P, 2, BANK], FP32)
        att_tok = sb("att_tok", [P, 16, DH], FP32)
        inv_den = sb("inv_den", [P, 16], FP32)

        work = sb("work", [P, P_SLOTS, HALF + EXPD], FP32)
        flat = work[:, :, :].rearrange("p a b -> p (a b)")

        def scratch(at, n, shape=None):
            v = flat[:, at:at + n]
            return v.rearrange("p (a b) -> p a b", b=shape) if shape else v

        def narrow(at, n, rows, dt):
            return coeff[0:rows, :, :].rearrange("p a b -> p (a b)")[:, at:at + n].bitcast(dt)

        x_in = narrow(0, 2 * GROUP, FRAME + 1, FP32)
        y = scratch(0, 1024, HID)
        x1 = scratch(2048, 1024, HID)
        x1t = scratch(3072, 1024, GROUP)
        q32 = scratch(4096, 1024, GROUP)
        sq = scratch(5120, 512).bitcast(BF16).rearrange("p (a b) -> p a b", b=GROUP)
        v_sb = scratch(6144, 1024, HID)
        ones_f = scratch(9216, FB * HEADS, HEADS)
        q16 = [scratch(7168, 512).bitcast(FP16).rearrange("p (a b) -> p a b", b=GROUP),
               scratch(7680, 512).bitcast(FP16).rearrange("p (a b) -> p a b", b=GROUP)]
        norm_sb = narrow(1024, 2 * GROUP, HEADS, FP32)
        q16_near = [scratch(8192, 512).bitcast(FP16).rearrange("p (a b) -> p a b", b=GROUP),
                    scratch(8704, 512).bitcast(FP16).rearrange("p (a b) -> p a b", b=GROUP)]
        bits = narrow(2048, GROUP, HEADS * BITS, FP16)
        code_sb = narrow(2560, GROUP, HEADS, BF16)
        stats = sb("stats", [P, SUB, 6], FP32)
        mv = sb("mv", [P, SUB, 2], FP32)
        var_e = sb("var_e", [P, SUB], FP32)
        rstd = sb("rstd", [P, SUB], FP32)

        x2, x2t = y, [scratch(1024, 1024, GROUP), scratch(4096, 1024, GROUP)]
        wax = scratch(2048, 512)
        w_exp = scratch(2560, 512)
        out_sb = scratch(3072, 1024, HID)
        logit = sb("logit", [P, SUB, EXPERTS], FP32)
        ranked = sb("ranked", [P, SUB, 8], FP32)
        e_w = sb("e_w", [P, SUB, EXPERTS], FP32)
        e_mask = sb("e_mask", [P, SUB, EXPERTS], FP32)
        e_sum = sb("e_sum", [P, SUB], FP32)
        e_inv = sb("e_inv", [P, SUB], FP32)
        w_t = narrow(3072, 2 * GROUP, EXPERTS, FP32)

        norms = flat[0:ALL_HEADS, 0:SEQ]
        mids = flat[0:ALL_HEADS, SEQ:2 * SEQ]
        nu16 = narrow(0, SEQ, ALL_HEADS, FP16)
        peak = sb("peak", [32, 32], FP32)
        peak_t = sb("peak_t", [32, 32], FP32)
        peak_all = sb("peak_all", [1, 1], FP32)
        flag = sb("flag", [1, 1], INT32)
        row_max4 = sb("row_max4", [P, 4], FP32)
        row_max = sb("row_max", [P, TT], FP32)
        nu_t = sb("nu_t", [TT, P], FP32)
        nu_t16 = sb("nu_t16", [TT, P], FP16)

        psum = ctx.enter_context(nc.psum_tensor("psum", [P, 8 * BANK], FP32))

        def banks(a, n, shape=None, rows=P):
            v = psum[0:rows, a * BANK:(a + n) * BANK]
            return v.rearrange("p (a b) -> p a b", b=shape) if shape else v

        hp, xtp, qp, vp = banks(0, 2, HID), banks(2, 2, GROUP), banks(4, 2, GROUP), banks(6, 2, HID)
        planes_p, norm_p = banks(0, 1, rows=HEADS * BITS), banks(1, 1, rows=HEADS)
        code_row_p, code_col_p = banks(2, 1, rows=HEADS), banks(3, 1)[:, 0:SUB * HEADS]
        x_slot = [banks(0, 2), banks(2, 2)]
        x_pair, x_single = banks(0, 2), [banks(2, 1), banks(3, 1)]
        x_masked, x_far, x_near = banks(4, 2), banks(4, 1), banks(5, 1)
        acc = [banks(6, 1), banks(7, 1)]
        x2tp, logit_p, w_tp = banks(0, 2, GROUP), banks(2, 1)[:, 0:SUB * EXPERTS], banks(3, 1, rows=EXPERTS)
        axt_p, w_exp_p, out_p = banks(4, 1), banks(5, 1), banks(6, 2, HID)

        first_in = sem("first_in")
        weights_in = sem("weights_in")
        consts_set = sem("consts_set")
        x_loaded = sem("x_loaded")
        tok_ready = sem("tok_ready")
        vec = sem("vec")
        vec_b = sem("vec_b")
        route = sem("route")
        var_ready = sem("var_ready")
        rstd_ready = sem("rstd_ready")
        y_ready = sem("y_ready")
        gained = sem("gained")
        gained_v = sem("gained_v")
        affine_ready = sem("affine_ready")
        gelu_ready = sem("gelu_ready")
        x1_ready = sem("x1_ready")
        x1t_psum = sem("x1t_psum")
        x1t_ready = sem("x1t_ready")
        q_psum = sem("q_psum")
        v_psum = sem("v_psum")
        q32_ready = sem("q32_ready")
        sq_ready = sem("sq_ready")
        v_ready = sem("v_ready")
        q16_ready = sem("q16_ready")
        planes_psum = sem("planes_psum")
        norm_psum = sem("norm_psum")
        bits_ready = sem("bits_ready")
        codes_psum = sem("codes_psum")
        norm_ready = sem("norm_ready")
        codes_ready = sem("codes_ready")
        q_stored = sem("q_stored")
        v_stored = sem("v_stored")
        code_stored = sem("code_stored")
        norm_stored = sem("norm_stored")
        norms_in = sem("norms_in")
        peak_ready = sem("peak_ready")
        mids_ready = sem("mids_ready")
        nu_ready = sem("nu_ready")
        nu_stored = sem("nu_stored")
        flag_ready = sem("flag_ready")
        gen_in = sem("gen_in")
        gen_scores = sem("gen_scores")
        gen_maxed = sem("gen_maxed")
        gen_turned = sem("gen_turned")
        gen_nu = sem("gen_nu")
        gen_vec = sem("gen_vec")
        gen_rows = sem("gen_rows")
        gen_zero = sem("gen_zero")
        gen_stored = sem("gen_stored")
        head_in = [sem(f"head_in{i}") for i in range(2)]
        onehots = sem("onehots")
        shift_rows = sem("shift_rows")
        code_col_ready = sem("code_col_ready")
        coeff_ready = sem("coeff_ready")
        pair_ready = sem("pair_ready")
        single_ready = sem("single_ready")
        masked_ready = sem("masked_ready")
        scaled = sem("scaled")
        masked_exp = sem("masked_exp")
        mixed = sem("mixed")
        probs_ready = sem("probs_ready")
        probs_used = sem("probs_used")
        acc_copied = sem("acc_copied")
        acc_turned = sem("acc_turned")
        acc_free = sem("acc_free")
        att_steps = sem("att_steps")
        att_added = sem("att_added")
        first_shifts = sem("first_shifts")
        based = sem("based")
        key_hots = sem("key_hots")
        f_x2 = sem("f_x2")
        f_x2t_psum = sem("f_x2t_psum")
        f_x2t = sem("f_x2t")
        f_logits = sem("f_logits")
        f_diff = sem("f_diff")
        f_exp = sem("f_exp")
        f_w = sem("f_w")
        f_wt_psum = sem("f_wt_psum")
        f_wt = sem("f_wt")
        f_wexp_psum = sem("f_wexp_psum")
        f_wexp = sem("f_wexp")
        f_wax = sem("f_wax")
        f_out_psum = sem("f_out_psum")
        f_out = sem("f_out")
        stored = sem("stored")

        POOL_TILES = SUB // 2
        FIRST_LOADS, WEIGHT_LOADS = 3, 17
        HEAD_LOADS = 15
        PIECE = 256
        PIECES = SEQ // PIECE + 12
        block = ctx.enter_context(nc.Block())

        def lag(eng, s, value):
            if not (isinstance(value, int) and value <= 0):
                eng.wait_ge(s, value)

        def over_groups(eng, body):
            body(0)
            with eng.Fori(1, GROUPS) as g:
                body(g)

        def two_stages(eng, ahead, both, behind):
            ahead(0)
            both(0)
            with eng.Fori(1, GROUPS - 1) as g:
                both(g)
            behind(GROUPS - 1)

        def after_groups(eng, body):
            body(0, 0, 2)
            body(1, 1, 2)
            with eng.Fori(1, GROUPS // 2 - 1) as two:
                body(two * 2, 0, 2)
                body(two * 2 + 1, 1, 2)
            body(GROUPS - 2, 0, 1)
            body(GROUPS - 1, 1, 0)

        @block.sync
        def _(sp):
            def wide(row):
                return row.rearrange("(a n) -> a n", a=1).broadcast_to((P, HID))

            for dst, src in (
                (wtok_sb[:, :], w_tok),
                (gamma_sb[:, :], wide(gamma)),
                (beta_sb[:, :], wide(beta)),
            ):
                sp.dma_start(dst, src).then_inc(first_in, 16)

            sp.wait_ge(consts_set, 1)

            def load_group(g):
                lag(sp, tok_ready, g)
                sp.dma_start(x_in[0:FRAME, :], x_t[:, bass.ds(g * GROUP, GROUP)]).then_inc(x_loaded, 16)

            def leave(g):
                sp.wait_ge(v_ready, g + 1)
                sp.wait_ge(q16_ready, g + 1)
                sp.wait_ge(norm_ready, g + 1)
                sp.wait_ge(codes_ready, g + 1)
                sp.dma_start(v_rows[bass.ds(g * GROUP, GROUP), :].rearrange("(k p) c -> p k c", p=P), v_sb).then_inc(v_stored, 16)
                for part in range(2):
                    sp.dma_start(q_parts[part, :, bass.ds(g * GROUP, GROUP)].rearrange("(f p) s -> p f s", p=P), q16[part]).then_inc(q_stored, 16)
                    sp.dma_start(q_near_parts[part, :, bass.ds(g * GROUP, GROUP)].rearrange("(f p) s -> p f s", p=P), q16_near[part]).then_inc(q_stored, 16)
                sp.dma_start(norm_rows[:, bass.ds(g * GROUP, GROUP)], norm_sb[:, :]).then_inc(norm_stored, 16)
                sp.dma_start(code_rows[:, bass.ds(g * GROUP, GROUP)], code_sb[:, :]).then_inc(code_stored, 16)

            load_group(0)
            for dst, src in (
                (wq_sb[:, :, :], wq_t.rearrange("(c p) n -> p c n", p=P)),
                (eye_sb[:, :], eye),
                (bq_sb[:, :], bq),
                (wv_sb[:, :, :], wv_t.rearrange("(c p) n -> p c n", p=P)),
                (bv_sb[:, :], wide(bv)),
                (ones_f, head_ones),
                (plane_sb[:, :, :], hyper.rearrange("(c p) n -> p c n", p=P)),
                (plane_b[:, :], hyper_b),
                (powers_sb[:, :], powers),
                (base_sb[:, :, :], base_w_t.rearrange("(c p) n -> p c n", p=P)),
                (lora_a_sb[:, :, :], lora_a.rearrange("(c p) n -> p c n", p=P)),
                (lora_b_sb[:, :], lora_b),
                (router_sb[:, :, :], router_t.rearrange("(c p) n -> p c n", p=P)),
                (base_b_sb[:, :], wide(base_b)),
                (router_b_row, router_b.rearrange("(a n) -> a n", a=1)),
                (bucket_col[:, :], bucket_of),
                (expert_sb[:, :], expert_rows),
            ):
                sp.dma_start(dst, src).then_inc(weights_in, 16)
            load_group(1)
            with sp.Fori(0, GROUPS - 2) as g:
                load_group(g + 2)
                leave(g)
            leave(GROUPS - 2)
            leave(GROUPS - 1)

            sp.wait_ge(norm_stored, 16 * GROUPS)
            sp.wait_ge(v_stored, 16 * GROUPS)
            sp.wait_ge(q_stored, 64 * GROUPS)
            sp.wait_ge(code_stored, 16 * GROUPS)
            for b in range(BATCH):
                sp.dma_start(norms[b * HEADS:(b + 1) * HEADS, :], norm_rows[:, b * SEQ:(b + 1) * SEQ]).then_inc(norms_in, 16)

            def operand_rows(k_dst, q_dst, h16, off, s):
                for i in range(4):
                    for dst, part in ((k_dst, i // 2), (q_dst, i % 2)):
                        sp.dma_start(dst[DH * i:DH * (i + 1), :],
                                     q_parts[part, bass.ds(h16, DH), bass.ds(off, SEQ)]).then_inc(s, 16)

            def load_rest(b, local, odd):
                s = head_in[odd]
                for i in range(4):
                    sp.dma_start(q_near[odd][DH * i:DH * (i + 1), :, :],
                                 q_near_parts[i % 2, bass.ds(local * DH, DH), bass.ds(b * SEQ, SEQ)].rearrange("d (a s) -> d a s", a=2)[:, :, MULT:HALF]).then_inc(s, 16)
                sp.dma_start(codes[odd][:, :], code_rows[bass.ds(local, 1), bass.ds(b * SEQ, SEQ)].broadcast_to((P, SEQ))).then_inc(s, 16)
                sp.dma_start(v_op[odd][:, :, 0:DH],
                             v_rows[bass.ds(b * SEQ, SEQ), bass.ds(local * DH, DH)].rearrange("(i p) d -> p i d", p=P)).then_inc(s, 16)

            load_rest(0, 0, 0)
            sp.wait_ge(flag_ready, 1)
            wide = sp.value_load(flag[0:1, 0:1], min_val=0, max_val=1)
            with sp.If(wide < 1):
                operand_rows(k_op[0], q_op[0], 0, 0, head_in[0])
                sp.wait_ge(nu_ready, 1)
                for b in range(BATCH):
                    sp.dma_start(nu_rows[:, b, :], nu16[b * HEADS:(b + 1) * HEADS, :]).then_inc(nu_stored, 16)
                sp.wait_ge(nu_stored, 16 * BATCH)
            with sp.Else():
                with sp.Fori(0, BATCH) as b:
                    with sp.Fori(0, HEADS) as local:
                        h = b * HEADS + local
                        sp.wait_ge(gen_nu, h + 1)
                        operand_rows(k_op[0], q_op[0], local * DH, b * SEQ, gen_in)
                        sp.wait_ge(gen_nu, h + 2)
                        sp.dma_start(nu_rows[bass.ds(local, 1), bass.ds(b, 1), :].rearrange("a b (i p) -> (a b i) p", p=P), nu_t16[:, :]).then_inc(nu_stored, 16)

                sp.wait_ge(nu_stored, 16 * ALL_HEADS)
                operand_rows(k_op[0], q_op[0], 0, 0, head_in[0])

            def load_head(b, local, odd, first=False):
                h = b * HEADS + local
                s = head_in[odd]
                if not first:
                    sp.wait_ge(probs_used, (h - 1) * HEAD_STEPS + P_SLOTS)
                if not (first and odd == 0):
                    operand_rows(k_op[odd], q_op[odd], local * DH, b * SEQ, s)
                    load_rest(b, local, odd)
                if not first:
                    sp.wait_ge(shift_rows, (h - 1) * PIECES)
                elif odd:
                    sp.wait_ge(first_shifts, 2)
                sp.dma_start(nu_b[P // 2:P, :], nu_rows[bass.ds(local, 1), bass.ds(b, 1), :].rearrange("a b s -> (a b) s").broadcast_to((P // 2, SEQ))).then_inc(s, 16)

            load_head(0, 0, 0, first=True)
            load_head(0, 1, 1, first=True)
            with sp.Fori(1, HEADS // 2) as pair:
                for odd in range(2):
                    load_head(0, pair * 2 + odd, odd)
            with sp.Fori(0, HEADS // 2) as pair:
                for odd in range(2):
                    load_head(1, pair * 2 + odd, odd)

            def out_group(g):
                sp.wait_ge(f_out, g + 1)
                sp.dma_start(out[bass.ds(g * GROUP, GROUP), :].rearrange("(k p) c -> p k c", p=P), out_sb).then_inc(stored, 16)
            with sp.Fori(0, GROUPS) as g:
                out_group(g)
            sp.wait_ge(stored, 16 * GROUPS)

        @block.gpsimd
        def _(pool):
            pool.memset(x_in[:, :], 1.0).then_inc(consts_set, 1)
            pool.memset(neg_half[:, :], -0.5).then_inc(consts_set, 1)
            pool.memset(ones_row, 1.0).then_inc(consts_set, 1)
            pool.wait_ge(consts_set, 3)
            pool.wait_ge(first_in, 16 * FIRST_LOADS)

            def inv_sqrt(n):
                pool.wait_ge(var_ready, n)
                pool.tensor_tensor(rstd[:, :], var_e[:, :], neg_half[:, :], ALU.pow).then_inc(rstd_ready, 1)

            def group(g):
                inv_sqrt(g * 2 + 1)
                pool.wait_ge(y_ready, g + 1)
                some = y[:, 0:POOL_TILES, :]
                pool.tensor_tensor(some, some, gamma_sb[:, :].unsqueeze(1).broadcast_to((P, POOL_TILES, HID)), ALU.mult).then_inc(gained, 1)
                pool.wait_ge(gained, g + 1)
                pool.tensor_tensor(some, some, beta_sb[:, :].unsqueeze(1).broadcast_to((P, POOL_TILES, HID)), ALU.add).then_inc(affine_ready, 1)
                inv_sqrt(g * 2 + 2)
            over_groups(pool, group)

            up = slice(P // 2, P)

            def piece(nth, odd, i):
                if i < SEQ // PIECE:
                    cols = slice(i * PIECE, (i + 1) * PIECE)
                    to = q_op[odd][up, cols]
                    ins = pool.tensor_tensor(to, to, nu_b[up, cols], ALU.mult)
                else:
                    at, what = divmod(i - SEQ // PIECE, 3)
                    c, q0 = at // 2, at % 2 * PIECE
                    cols = slice(q0, q0 + PIECE)
                    all_cols = slice(c * HALF + MULT + q0, c * HALF + MULT + q0 + PIECE)
                    near = q_near[odd][up, c, cols]
                    if what == 0:
                        ins = pool.tensor_tensor(near, nu_b[up, all_cols], neg_near[up, :], ALU.mult)
                    elif what == 1:
                        ins = pool.tensor_tensor(near, near, near_add[up, c, cols], ALU.add)
                    else:
                        std = q_op[odd][up, all_cols]
                        ins = pool.tensor_tensor(std, std, far_add[up, c, cols], ALU.add)
                ins.then_inc(shift_rows, 1)
                pool.wait_ge(shift_rows, nth * PIECES + (i + 1))

            def add_attended(rounds, half, b, local):
                pool.wait_ge(acc_free, rounds + 3)
                rows = hidden[:, bass.ds(b * TT + half * 16, 16), bass.ds(local * DH, DH)]
                pool.tensor_tensor(rows, rows, att_tok[:, :, :], ALU.add).then_inc(att_added, 1)

            FIRST_PIECE = 20
            with pool.Fori(0, BATCH) as b:
                with pool.Fori(0, HEADS // 2) as p:
                    pair = b * (HEADS // 2) + p
                    for n in range(STEPS):
                        pool.wait_ge(masked_exp, pair * STEPS + (n + 2))
                        to = work[:, n % P_SLOTS, MULT:HALF]
                        pool.tensor_tensor(to, to, work[:, n % P_SLOTS, HALF:], ALU.add).then_inc(mixed, 1)
                        if FIRST_PIECE <= n < FIRST_PIECE + PIECES:
                            pool.wait_ge(mixed, pair * STEPS + (n + 1))
                            if n == FIRST_PIECE:
                                pool.wait_ge(onehots, pair * 2 + 2)
                            piece(pair * 2, 1, n - FIRST_PIECE)
                        if HEAD_STEPS + FIRST_PIECE <= n < HEAD_STEPS + FIRST_PIECE + PIECES:
                            with pool.If(pair < ALL_HEADS // 2 - 1):
                                pool.wait_ge(mixed, pair * STEPS + (n + 1))
                                if n == HEAD_STEPS + FIRST_PIECE:
                                    pool.wait_ge(onehots, pair * 2 + 3)
                                piece(pair * 2 + 1, 0, n - HEAD_STEPS - FIRST_PIECE)
                        if n == 12:
                            with pool.If(p > 0):
                                add_attended(pair * 4 - 1, 1, b, (p * 2 + HEADS - 1) & (HEADS - 1))
                            with pool.Else():
                                with pool.If(b > 0):
                                    add_attended(pair * 4 - 1, 1, 0, HEADS - 1)
                        elif n % TT == 12:
                            r = n // TT - 1
                            add_attended(pair * 4 + r, r % 2, b, p * 2 + r // 2)
            add_attended(2 * ALL_HEADS - 1, 1, 1, HEADS - 1)

            def add_base_bias(g):
                inv_sqrt(g + 2 * GROUPS + 1)
                pool.wait_ge(f_x2, g + 1)
                rows = hidden[:, bass.ds(g * SUB, SUB), :]
                pool.tensor_tensor(rows, rows, base_b_sb[:, :].unsqueeze(1).broadcast_to((P, SUB, HID)), ALU.add).then_inc(based, 1)
            with pool.Fori(0, GROUPS) as g:
                add_base_bias(g)

        @block.scalar
        def _(act):
            def gelu(g):
                act.wait_ge(affine_ready, g * 2 + 2)
                act.activation(hidden[:, bass.ds(g * SUB, SUB), :], y, ACT.Gelu).then_inc(gelu_ready, 1)

            def squares(g):
                act.wait_ge(q32_ready, g * FB + FB)
                act.activation(sq, q32, ACT.Square, scale=QS).then_inc(sq_ready, 1)

            def queries(g):
                act.wait_ge(x1t_psum, g + 1)
                act.activation(x1t, xtp, ACT.Copy).then_inc(x1t_ready, 1)
                act.wait_ge(q_psum, g + 1)
                for f in range(FB):
                    act.activation(q32[:, f, :], qp[:, f, :], ACT.Identity, bias=bq_sb[:, f:f + 1]).then_inc(q32_ready, 1)

            def ahead(g):
                gelu(g)
                act.wait_ge(weights_in, 16 * WEIGHT_LOADS)

            def both(g):
                queries(g)
                gelu(g + 1)
                squares(g)

            def behind(g):
                queries(g)
                squares(g)
            two_stages(act, ahead, both, behind)

            act.wait_ge(peak_ready, 1)
            act.activation(mids, norms, ACT.Sqrt, scale=peak[:, 0:1]).then_inc(mids_ready, 1)

            def copy_acc(rounds, half):
                act.wait_ge(probs_used, rounds * TT + P_SLOTS + TT)
                act.wait_ge(acc_turned, rounds + 1)
                act.activation(att_sb[:, half, :], acc[half], ACT.Copy).then_inc(acc_copied, 1)

            with act.Fori(0, ALL_HEADS // 2) as pair:
                for n in range(STEPS):
                    act.wait_ge(probs_used, pair * STEPS + (n + 1))
                    act.wait_ge(masked_ready, pair * STEPS + (n + 1))
                    act.activation(work[:, n % P_SLOTS, MULT:], x_masked, ACT.Exp, scale=FAR * SCORE).then_inc(masked_exp, 1)
                    act.wait_ge(scaled, pair * (2 * STEPS) + (2 * n + 5))
                    act.activation(work[:, n % P_SLOTS, 0:MULT], work[:, n % P_SLOTS, 0:MULT], ACT.Exp, scale=SCORE).then_inc(probs_ready, 1)
                    if n == 3:
                        with act.If(pair > 0):
                            copy_acc(pair * 4 - 1, 1)
                    elif n % TT == 3:
                        copy_acc(pair * 4 + (n // TT - 1), (n // TT - 1) % 2)
            copy_acc(2 * ALL_HEADS - 1, 1)

            def turned(g, par):
                act.wait_ge(f_x2t_psum, g + 1)
                act.activation(x2t[par], x2tp, ACT.Copy).then_inc(f_x2t, 1)

            def route_exp(g):
                act.wait_ge(f_diff, g + 1)
                act.activation(e_w[:, :, :], e_w[:, :, :], ACT.Exp).then_inc(f_exp, 1)

            def weights_turned(g):
                act.wait_ge(f_wt_psum, g + 1)
                act.activation(w_t[:, :], w_tp, ACT.Copy).then_inc(f_wt, 1)

            def weights_wide(g):
                act.wait_ge(f_wexp_psum, g + 1)
                act.activation(w_exp, w_exp_p, ACT.Copy).then_inc(f_wexp, 1)

            def after(g, par, more):
                weights_turned(g)
                if more:
                    turned(g + 1, 1 - par)
                    route_exp(g + 1)
                weights_wide(g)
            turned(0, 0)
            route_exp(0)
            after_groups(act, after)

        @block.tensor
        def _(pe):
            pe.wait_ge(first_in, 16 * FIRST_LOADS)
            pe.wait_ge(consts_set, 3)

            def tokens(g):
                pe.wait_ge(x_loaded, g * 16 + 16)
                lag(pe, y_ready, g)
                lag(pe, norm_ready, g - 1)
                for k in range(SUB):
                    mm = pe.matmul(hp[:, k, :], x_in[:, k * P:(k + 1) * P], wtok_sb[:, :], start=True, stop=True)
                mm.then_inc(tok_ready, 1)

            def project(g, ahead):
                pe.wait_ge(x1_ready, g + 1)
                lag(pe, codes_ready, g)
                for k in range(SUB):
                    for f in range(FB):
                        mm = pe.transpose(xtp[:, f, k * P:(k + 1) * P], x1[:, k, f * P:(f + 1) * P], eye_sb[:, :])
                mm.then_inc(x1t_psum, 1)
                pe.wait_ge(x1t_ready, g + 1)
                lag(pe, q32_ready, g * FB)
                for f in range(FB):
                    for c in range(FB):
                        mm = pe.matmul(qp[:, f, :], wq_sb[:, c, f * P:(f + 1) * P], x1t[:, c, :], start=(c == 0), stop=(c == FB - 1))
                mm.then_inc(q_psum, 1)
                lag(pe, v_ready, g)
                for k in range(SUB):
                    for c in range(FB):
                        mm = pe.matmul(vp[:, k, :], x1t[:, c, k * P:(k + 1) * P], wv_sb[:, c, :], start=(c == 0), stop=(c == FB - 1))
                mm.then_inc(v_psum, 1)
                pe.wait_ge(q32_ready, g * FB + FB)
                pe.wait_ge(y_ready, g + 1 + ahead)
                for f in range(FB):
                    mm = pe.matmul(planes_p, plane_sb[:, f, :], q32[:, f, :], start=(f == 0), stop=(f == FB - 1))
                mm.then_inc(planes_psum, 1)
                pe.wait_ge(sq_ready, g + 1)
                for f in range(FB):
                    mm = pe.matmul(norm_p, ones_h[:, f, :], sq[:, f, :], start=(f == 0), stop=(f == FB - 1))
                mm.then_inc(norm_psum, 1)
                pe.wait_ge(bits_ready, g + 1)
                pe.matmul(code_row_p, powers_sb[:, :], bits[:, :], start=True, stop=True)
                for k in range(SUB):
                    mm = pe.matmul(code_col_p[:, k * HEADS:(k + 1) * HEADS], bits[:, k * P:(k + 1) * P], powers_sb[:, :], start=True, stop=True)
                mm.then_inc(codes_psum, 1)

            def both(g):
                tokens(g + 1)
                project(g, 1)

            def ahead(g):
                tokens(g)
                pe.wait_ge(weights_in, 16 * WEIGHT_LOADS)
                pe.wait_ge(consts_set, 4)
            two_stages(pe, ahead, both, lambda g: project(g, 0))

            pe.wait_ge(flag_ready, 1)
            wide = pe.value_load(flag[0:1, 0:1], min_val=0, max_val=1)
            with pe.If(wide > 0):
                pe.wait_ge(gen_zero, 2)
                with pe.Fori(0, ALL_HEADS) as h:
                    with pe.Fori(0, TT) as i:
                        pe.wait_ge(gen_in, h * (8 * 16) + 8 * 16)
                        for c in range(4):
                            n = (h * TT + i) * 4 + c
                            pe.wait_ge(gen_maxed, n + 1)
                            for j in range(2):
                                mm = pe.matmul(x_slot[c % 2][:, j * BANK:(j + 1) * BANK], q_op[0][:, bass.ds(i * P, P)],
                                               k_op[0][:, c * CHUNK + j * BANK:c * CHUNK + (j + 1) * BANK], start=True, stop=True)
                            mm.then_inc(gen_scores, 1)
                    pe.wait_ge(gen_rows, h * TT + TT)
                    pe.transpose(psum[0:TT, 4 * BANK:4 * BANK + P], row_max[:, :], eye_sb[:, :]).then_inc(gen_turned, 1)

            def scores(pair, n):
                odd, half, t = n // HEAD_STEPS, n // TT % 2, n % TT
                keys = k_op[odd][:, t * P:(t + 1) * P]
                pe.wait_ge(scaled, pair * (2 * STEPS) + (2 * n + 2))
                for j in range(2):
                    q0 = half * HALF + j * BANK
                    mm = pe.matmul(x_pair[:, j * BANK:(j + 1) * BANK], keys, q_op[odd][:, q0:q0 + BANK], start=True, stop=True)
                mm.then_inc(pair_ready, 1)
                q0 = half * HALF + CHUNK
                pe.matmul(x_single[n % 2], keys, q_op[odd][:, q0:q0 + BANK], start=True, stop=True).then_inc(single_ready, 1)

            def masked_scores(pair, n):
                odd, half, t = n // HEAD_STEPS, n // TT % 2, n % TT
                keys = k_op[odd][:, t * P:(t + 1) * P]
                pe.wait_ge(masked_exp, pair * STEPS + (n + 1))
                pe.matmul(x_far, keys, q_op[odd][:, half * HALF + MULT:(half + 1) * HALF], start=True, stop=True)
                pe.matmul(x_near, keys, q_near[odd][:, half, :], start=True, stop=True).then_inc(masked_ready, 1)

            def values(pair, n):
                odd, half, t = n // HEAD_STEPS, n // TT % 2, n % TT
                if t == 0:
                    pe.wait_ge(acc_free, pair * 4 + (n // TT + 1))
                pe.wait_ge(probs_ready, pair * STEPS + (n + 1))
                pe.wait_ge(mixed, pair * STEPS + (n + 1))
                for j in range(4):
                    mm = pe.matmul(acc[half][32 * j:32 * (j + 1), :], v_op[odd][:, t, :], work[:, n % P_SLOTS, j * BANK:(j + 1) * BANK],
                                   start=(t == 0), stop=(t == TT - 1), tile_position=(0, 32 * j))
                mm.then_inc(probs_used, 1)

            def turn(rounds, half):
                pe.wait_ge(acc_copied, rounds + 1)
                for i in range(4):
                    mm = pe.transpose(acc[half][:, i * P:(i + 1) * P], att_sb[:, half, i * P:(i + 1) * P], eye_sb[:, :])
                mm.then_inc(acc_turned, 1)

            pe.wait_ge(first_shifts, 3)
            for n in range(2):
                scores(0, n)
                masked_scores(0, n)
            with pe.Fori(0, ALL_HEADS // 2) as pair:
                for n in range(STEPS):
                    if n + 2 == HEAD_STEPS:
                        pe.wait_ge(shift_rows, pair * (2 * PIECES) + PIECES)
                    if n + 2 < STEPS:
                        scores(pair, n + 2)
                        values(pair, n)
                        masked_scores(pair, n + 2)
                    else:
                        if n + 2 == STEPS:
                            with pe.If(pair < ALL_HEADS // 2 - 1):
                                pe.wait_ge(shift_rows, pair * (2 * PIECES) + 2 * PIECES)
                                scores(pair + 1, 0)
                        values(pair, n)
                        with pe.If(pair < ALL_HEADS // 2 - 1):
                            if n + 1 == STEPS:
                                scores(pair + 1, 1)
                            masked_scores(pair + 1, n + 2 - STEPS)
                    if n == 4:
                        with pe.If(pair > 0):
                            turn(pair * 4 - 1, 1)
                    elif n % TT == 4:
                        turn(pair * 4 + (n // TT - 1), (n // TT - 1) % 2)
            turn(2 * ALL_HEADS - 1, 1)

            def route_scores(g, par):
                pe.wait_ge(f_x2, g + 1)
                for k in range(SUB):
                    for f in range(FB):
                        mm = pe.transpose(x2tp[:, f, k * P:(k + 1) * P], x2[:, k, f * P:(f + 1) * P], eye_sb[:, :])
                mm.then_inc(f_x2t_psum, 1)
                pe.wait_ge(f_x2t, g + 1)
                for k in range(SUB):
                    to = logit_p[:, k * EXPERTS:(k + 1) * EXPERTS]
                    for c in range(FB):
                        pe.matmul(to, x2t[par][:, c, k * P:(k + 1) * P], router_sb[:, c, :], start=(c == 0), stop=False)
                    mm = pe.matmul(to, ones_row, router_b_row, start=False, stop=True)
                mm.then_inc(f_logits, 1)

            def after(g, par, more):
                pe.wait_ge(f_w, g + 1)
                for k in range(SUB):
                    mm = pe.transpose(w_tp[:, k * P:(k + 1) * P], e_w[:, k, :], eye_sb[:, :])
                mm.then_inc(f_wt_psum, 1)
                if more:
                    route_scores(g + 1, 1 - par)
                for c in range(FB):
                    pe.matmul(axt_p, lora_a_sb[:, c, :], x2t[par][:, c, :], start=(c == 0), stop=(c == FB - 1))
                pe.wait_ge(f_wt, g + 1)
                pe.matmul(w_exp_p, expert_sb[:, :], w_t[:, :], start=True, stop=True).then_inc(f_wexp_psum, 1)
                lag(pe, f_out, g)
                for k in range(SUB):
                    for c in range(FB):
                        pe.matmul(out_p[:, k, :], x2t[par][:, c, k * P:(k + 1) * P], base_sb[:, c, :], start=(c == 0), stop=False)
                    if k == 0:
                        pe.wait_ge(f_wax, g + 1)
                    mm = pe.matmul(out_p[:, k, :], wax[:, k * P:(k + 1) * P], lora_b_sb[:, :], start=False, stop=True)
                mm.then_inc(f_out_psum, 1)
            route_scores(0, 0)
            after_groups(pe, after)

        @block.vector
        def _(dve):
            LN_STEPS = 2 + 2 * SUB + SUB - 1
            ROUTE_STEPS = SUB + 6

            def apart(s):
                s.mark(dve.memset(wait_carrier[:, :], 0.0))

            def norm_stats(s, src, eps):
                apart(s)
                for k in range(SUB):
                    at = s.mark(dve.bn_stats(stats[:, k, :], src(k)))
                s.wait(at)
                apart(s)
                for k in range(SUB):
                    at = s.mark(dve.bn_aggr(mv[:, k, :], stats[:, k, :]))
                s.wait(at)
                dve.tensor_scalar(var_e[:, :], mv[:, :, 1], eps, None, ALU.add).then_inc(var_ready, 1)

            def normalise(s, dst, src, done):
                for k in range(SUB):
                    ins = dve.tensor_scalar(dst(k), src(k), mv[:, k, 0:1], rstd[:, k:k + 1], ALU.subtract, ALU.mult)
                    if k < SUB - 1:
                        s.mark(ins)
                ins.then_inc(done, 1)

            for i in range(2):
                dve.memset(v_op[i][:, :, :], 0.0).then_inc(vec, 1)
            dve.memset(peak[:, :], 0.0).then_inc(vec, 1)
            dve.wait_ge(vec, 3)
            for i in range(2):
                dve.memset(v_op[i][:, :, DH:DH + 1], 1.0).then_inc(vec, 1)
            dve.wait_ge(vec, 5)
            VEC0 = 5

            def hidden_rows(g):
                return lambda k: hidden[:, bass.ds(g * SUB + k, 1), :].rearrange("p a c -> p (a c)")

            def tokens(g):
                s = Steps(dve, vec, g * (2 * LN_STEPS) + VEC0)
                dve.wait_ge(tok_ready, g + 1)
                norm_stats(s, lambda k: hp[:, k, :], LN_EPS)
                dve.wait_ge(rstd_ready, g * 2 + 1)
                normalise(s, lambda k: y[:, k, :], lambda k: hp[:, k, :], y_ready)
                assert s.n == LN_STEPS
                some = y[:, POOL_TILES:, :]
                dve.wait_ge(y_ready, g + 1)
                dve.tensor_tensor(some, some, gamma_sb[:, :].unsqueeze(1).broadcast_to((P, SUB - POOL_TILES, HID)), ALU.mult).then_inc(gained_v, 1)
                dve.wait_ge(gained_v, g + 1)
                dve.tensor_tensor(some, some, beta_sb[:, :].unsqueeze(1).broadcast_to((P, SUB - POOL_TILES, HID)), ALU.add).then_inc(affine_ready, 1)

            def attention_input(g, meanwhile=None):
                s = Steps(dve, vec, g * (2 * LN_STEPS) + (VEC0 + LN_STEPS))
                dve.wait_ge(gelu_ready, g + 1)
                norm_stats(s, hidden_rows(g), LN_EPS)
                if meanwhile:
                    meanwhile()
                dve.wait_ge(rstd_ready, g * 2 + 2)
                normalise(s, lambda k: x1[:, k, :], hidden_rows(g), x1_ready)
                assert s.n == LN_STEPS

            def split_queries(g):
                dve.wait_ge(q32_ready, g * FB + FB)
                lag(dve, q_stored, g * 64)
                dve.tensor_scalar(q16[0], q32, QS, None, ALU.mult).then_inc(vec_b, 1)
                dve.tensor_scalar(q16_near[0], q32, QS * NEAR / FAR, None, ALU.mult).then_inc(vec_b, 1)

            def low_parts(g):
                dve.wait_ge(vec_b, g * 3 + 2)
                dve.scalar_tensor_tensor(q16[1], q32, QS, q16[0], ALU.mult, ALU.subtract)

            def near_low_parts(g):
                dve.wait_ge(vec_b, g * 3 + 2)
                dve.scalar_tensor_tensor(q16_near[1], q32, QS * NEAR / FAR, q16_near[0], ALU.mult, ALU.subtract).then_inc(q16_ready, 1)

            def group_values(g):
                dve.wait_ge(v_psum, g + 1)
                lag(dve, v_stored, g * 16)
                dve.tensor_tensor(v_sb, vp, bv_sb[:, :].unsqueeze(1).broadcast_to((P, SUB, HID)), ALU.add).then_inc(v_ready, 1)

            def buckets(g):
                dve.wait_ge(planes_psum, g + 1)
                dve.tensor_scalar(bits[:, :], planes_p, plane_b[:, 0:1], 0.0, ALU.add, ALU.is_ge).then_inc(bits_ready, 1)
                dve.wait_ge(norm_psum, g + 1)
                lag(dve, norm_stored, g * 16)
                dve.tensor_copy(norm_sb[:, :], norm_p).then_inc(norm_ready, 1)
                dve.wait_ge(codes_psum, g + 1)
                lag(dve, code_stored, g * 16)
                dve.tensor_copy(code_sb[:, :], code_row_p).then_inc(vec_b, 1)
                dve.tensor_copy(code_cols[:, bass.ds(g * SUB, SUB), :], code_col_p.rearrange("p (k h) -> p k h", h=HEADS)).then_inc(codes_ready, 1)

            def ahead(g):
                tokens(g)
                attention_input(g)
                dve.wait_ge(weights_in, 16 * WEIGHT_LOADS)
                dve.tensor_copy(ones_h[:, :, :], ones_f).then_inc(consts_set, 1)

            def both(g):
                tokens(g + 1)
                split_queries(g)
                attention_input(g + 1, lambda: low_parts(g))
                group_values(g)
                near_low_parts(g)
                buckets(g)

            def behind(g):
                split_queries(g)
                low_parts(g)
                near_low_parts(g)
                group_values(g)
                buckets(g)
            two_stages(dve, ahead, both, behind)

            VEC1 = VEC0 + 2 * LN_STEPS * GROUPS
            s = Steps(dve, vec, VEC1)
            dve.wait_ge(norms_in, 16 * BATCH)
            dve.tensor_reduce(peak[:, 0:1], norms, AX.X, ALU.max).then_inc(peak_ready, 1)
            dve.wait_ge(peak_ready, 1)
            s.wait(s.mark(dve.transpose(peak_t[:, :], peak[:, :])))
            s.wait(s.mark(dve.tensor_reduce(peak_all[:, :], peak_t[0:1, :], AX.X, ALU.max)))
            s.wait(s.mark(dve.tensor_scalar(peak_all[:, :], peak_all[:, :], -1.0 if force_general else SAFE, None, ALU.is_le)))
            dve.tensor_scalar(flag[:, :], peak_all[:, :], -1.0, 1.0, ALU.mult, ALU.add).then_inc(flag_ready, 1)
            dve.wait_ge(mids_ready, 1)
            s.wait(s.mark(dve.tensor_tensor(mids, mids, norms, ALU.add)))
            s.wait(s.mark(dve.tensor_scalar(mids, mids, 0.5 / NEAR, None, ALU.mult)))
            s.wait(s.mark(dve.tensor_single_scalar(mids.bitcast(INT32), mids.bitcast(INT32), KEEP_5_BITS, ALU.bitwise_and)))
            dve.tensor_copy(nu16, mids).then_inc(nu_ready, 1)
            dve.wait_ge(nu_ready, 1)
            VEC2 = VEC1 + s.n

            wide = dve.value_load(flag[0:1, 0:1], min_val=0, max_val=1)
            with dve.If(wide > 0):
                dve.memset(x_slot[0], 0.0).then_inc(gen_maxed, 1)
                dve.memset(x_slot[1], 0.0).then_inc(gen_maxed, 1)
                dve.memset(q_op[0][P // 2:P, :], 0.0).then_inc(gen_zero, 1)
                dve.memset(k_op[0][P // 2:P, :], 0.0).then_inc(gen_zero, 1)
                dve.memset(nu_t16[:, :], 0.0).then_inc(gen_nu, 1)
                with dve.Fori(0, ALL_HEADS) as h:
                    with dve.Fori(0, TT) as i:
                        for c in range(4):
                            n = (h * TT + i) * 4 + c
                            dve.wait_ge(gen_scores, n + 1)
                            dve.tensor_reduce(row_max4[:, c:c + 1], x_slot[c % 2], AX.X, ALU.max).then_inc(gen_maxed, 1)
                        dve.wait_ge(gen_maxed, (h * TT + i) * 4 + 6)
                        dve.tensor_reduce(row_max[:, bass.ds(i, 1)], row_max4[:, :], AX.X, ALU.max).then_inc(gen_rows, 1)
                        dve.wait_ge(gen_rows, h * TT + i + 1)
                    dve.wait_ge(gen_turned, h + 1)
                    g2 = Steps(dve, gen_vec, h * 2)
                    g2.wait(g2.mark(dve.tensor_scalar(nu_t[:, :], psum[0:TT, 4 * BANK:4 * BANK + P], 1.0625 / FAR, None, ALU.mult)))
                    g2.wait(g2.mark(dve.tensor_single_scalar(nu_t[:, :].bitcast(INT32), nu_t[:, :].bitcast(INT32), KEEP_5_BITS, ALU.bitwise_and)))
                    dve.tensor_copy(nu_t16[:, :], nu_t[:, :]).then_inc(gen_nu, 1)
                    dve.wait_ge(nu_stored, h * 16 + 16)
            with dve.Else():
                dve.wait_ge(nu_stored, 16 * BATCH)

            for bank in (x_pair, *x_single):
                dve.memset(bank[:, 0:1], 0.0).then_inc(scaled, 1)
            dve.memset(x_masked[:, 0:1], 0.0).then_inc(masked_exp, 1)
            dve.memset(neg_near[:, :], -NEAR).then_inc(att_steps, 1)
            dve.memset(inv_den[:, :], 0.0).then_inc(att_steps, 1)
            dve.memset(att_tok[:, :, :], 0.0).then_inc(att_added, 1)
            for i in range(P_SLOTS):
                dve.memset(work[:, i, 0:1], 0.0).then_inc(probs_used, 1)
            for i in range(2):
                dve.memset(acc[i][:, 0:1], 0.0).then_inc(acc_free, 1)
                dve.memset(att_sb[:, i, 0:1], 0.0).then_inc(acc_turned, 1)

            def onehot(nth, odd, b, local):
                dve.wait_ge(head_in[odd], nth * (16 * HEAD_LOADS) + 16 * HEAD_LOADS)
                up = slice(P // 2, P)
                dve.tensor_scalar(k_op[odd][up, :], codes[odd][up, :], bucket_col[up, 0:1], None, ALU.is_equal).then_inc(key_hots, 1)
                last = codes[odd][up, :].rearrange("p (a s) -> p a s", a=2)[:, :, MULT:HALF]
                dve.tensor_scalar(near_add[up, :, :], last, bucket_col[up, 0:1], -BIG, ALU.not_equal, ALU.mult).then_inc(key_hots, 1)
                dve.tensor_scalar(far_add[up, :, :], last, bucket_col[up, 0:1], -BIG, ALU.is_equal, ALU.mult).then_inc(key_hots, 1)
                dve.tensor_scalar(q_op[odd][up, :], codes[odd][up, :], bucket_col[up, 0:1], NEAR, ALU.is_equal, ALU.subtract).then_inc(onehots, 1)
                dve.tensor_copy(code_col[odd][:, :], code_cols[:, bass.ds(b * TT, TT), bass.ds(local, 1)].rearrange("p i a -> p (i a)")).then_inc(code_col_ready, 1)

            def first_head():
                up = slice(P // 2, P)
                s = Steps(dve, key_hots, 3)
                lasts = [t[up, :].rearrange("p (a s) -> p a s", a=2)[:, :, MULT:HALF] for t in (q_op[0], nu_b)]
                dve.wait_ge(onehots, 1)
                dve.wait_ge(key_hots, 3)
                dve.tensor_tensor(q_op[0][up, :], q_op[0][up, :], nu_b[up, :], ALU.mult).then_inc(first_shifts, 1)
                s.wait(s.mark(dve.tensor_scalar(q_near[0][up, :, :], lasts[1], -NEAR, None, ALU.mult)))
                dve.tensor_tensor(q_near[0][up, :, :], q_near[0][up, :, :], near_add[up, :, :], ALU.add).then_inc(first_shifts, 1)
                dve.wait_ge(first_shifts, 1)
                dve.tensor_tensor(lasts[0], lasts[0], far_add[up, :, :], ALU.add).then_inc(first_shifts, 1)

            def coefficient(pair, n):
                odd, half, t = n // HEAD_STEPS, n // TT % 2, n % TT
                if t == 0 and half == 0:
                    dve.wait_ge(code_col_ready, pair * 2 + (odd + 1))
                dve.tensor_scalar(coeff[:, n % C_SLOTS, :], codes[odd][:, half * HALF:half * HALF + MULT], code_col[odd][:, t:t + 1],
                                  FAR, ALU.is_equal, ALU.add).then_inc(coeff_ready, 1)

            def sums_inverted(rounds, half):
                dve.wait_ge(acc_turned, rounds + 3)
                dve.reciprocal(inv_den[:, :].rearrange("p (j i) -> p j i", j=4), turned_acc(half)[:, :, :, DH]).then_inc(att_steps, 1)

            def attended(rounds, half):
                dve.wait_ge(att_steps, rounds + 3)
                dve.wait_ge(att_added, rounds + 1)
                dve.tensor_tensor(att_tok[:, :, :].rearrange("p (j i) d -> p j i d", j=4), turned_acc(half)[:, :, :, 0:DH],
                                  inv_den[:, :].rearrange("p (j i) -> p j i", j=4).unsqueeze(3).broadcast_to((P, 4, 4, DH)), ALU.mult).then_inc(acc_free, 1)

            def turned_acc(half):
                return acc[half].rearrange("p (i j d) -> p j i d", j=4, d=32)

            onehot(0, 0, 0, 0)
            first_head()

            def scale(pair, n, tile, q0, width):
                dve.tensor_tensor(work[:, n % P_SLOTS, q0:q0 + width], tile, coeff[:, n % C_SLOTS, q0:q0 + width], ALU.mult).then_inc(scaled, 1)

            def head_pair(pair, b, p):
                dve.wait_ge(scaled, pair * (2 * STEPS) + 3)
                coefficient(pair, 0)
                for n in range(STEPS):
                    if n + 1 < STEPS:
                        if n >= 2:
                            dve.wait_ge(scaled, pair * (2 * STEPS) + (2 * n + 1))
                        coefficient(pair, n + 1)
                    dve.wait_ge(probs_used, pair * STEPS + (n + 1))
                    dve.wait_ge(coeff_ready, pair * STEPS + (n + 1))
                    dve.wait_ge(pair_ready, pair * STEPS + (n + 1))
                    scale(pair, n, x_pair, 0, CHUNK)
                    dve.wait_ge(single_ready, pair * STEPS + (n + 1))
                    scale(pair, n, x_single[n % 2], CHUNK, BANK)
                    for at, what in ((8, sums_inverted), (9, attended)):
                        if n == at:
                            with dve.If(pair > 0):
                                what(pair * 4 - 1, 1)
                        elif n % TT == at:
                            r = n // TT - 1
                            what(pair * 4 + r, r % 2)
                    if n == 12:
                        onehot(pair, 1, b, p * 2 + 1)
                    if n == HEAD_STEPS + 12:
                        with dve.If(p < HEADS // 2 - 1):
                            onehot(pair + 1, 0, b, (p * 2 + 2) & (HEADS - 1))
                        with dve.Else():
                            with dve.If(b < 1):
                                onehot(pair + 1, 0, 1, 0)

            with dve.Fori(0, BATCH) as b:
                with dve.Fori(0, HEADS // 2) as p:
                    head_pair(b * (HEADS // 2) + p, b, p)
            sums_inverted(2 * ALL_HEADS - 1, 1)
            attended(2 * ALL_HEADS - 1, 1)
            dve.wait_ge(att_added, 2 * ALL_HEADS + 1)

            def experts_input(g):
                s = Steps(dve, vec, g * LN_STEPS + VEC2)
                norm_stats(s, hidden_rows(g), LN_EPS)
                dve.wait_ge(rstd_ready, g + 2 * GROUPS + 1)
                normalise(s, lambda k: x2[:, k, :], hidden_rows(g), f_x2)
                assert s.n == LN_STEPS

            def routing(g):
                s = Steps(dve, route, g * ROUTE_STEPS)
                dve.wait_ge(f_logits, g + 1)
                s.wait(s.mark(dve.tensor_copy(logit[:, :, :], logit_p.rearrange("p (k e) -> p k e", e=EXPERTS))))
                apart(s)
                for k in range(SUB):
                    at = s.mark(dve.max(ranked[:, k, :], logit[:, k, :]))
                s.wait(at)
                dve.tensor_tensor(e_w[:, :, :], logit[:, :, :], ranked[:, :, 0:1].broadcast_to((P, SUB, EXPERTS)), ALU.subtract).then_inc(f_diff, 1)
                at = s.mark(dve.tensor_tensor(e_mask[:, :, :], logit[:, :, :], ranked[:, :, 1:2].broadcast_to((P, SUB, EXPERTS)), ALU.is_ge))
                dve.wait_ge(f_exp, g + 1)
                s.wait(at)
                s.wait(s.mark(dve.tensor_tensor(e_mask[:, :, :], e_w[:, :, :], e_mask[:, :, :], ALU.mult)))
                s.wait(s.mark(dve.tensor_reduce(e_sum[:, :], e_mask[:, :, :], AX.X, ALU.add)))
                s.wait(s.mark(dve.reciprocal(e_inv[:, :], e_sum[:, :])))
                dve.scalar_tensor_tensor(e_w[:, :, :], e_mask[:, :, :], LORA_SCALE, e_inv[:, :].unsqueeze(2).broadcast_to((P, SUB, EXPERTS)), ALU.mult, ALU.mult).then_inc(f_w, 1)
                assert s.n == ROUTE_STEPS

            def after(g, par, more):
                if more:
                    routing(g + 1)
                dve.wait_ge(f_wexp, g + 1)
                dve.tensor_tensor(wax, axt_p, w_exp, ALU.mult).then_inc(f_wax, 1)
                if more == 2:
                    experts_input(g + 2)
                dve.wait_ge(f_out_psum, g + 1)
                lag(dve, stored, g * 16)
                dve.wait_ge(based, g + 1)
                dve.tensor_tensor(out_sb, out_p, hidden[:, bass.ds(g * SUB, SUB), :], ALU.add).then_inc(f_out, 1)
            experts_input(0)
            routing(0)
            experts_input(1)
            after_groups(dve, after)


def kernel(**inputs):
    import numpy as _np
    import concourse.bacc as _bacc
    from concourse import mybir as _mybir
    from concourse.bass_utils import run_bass_kernel_spmd as _run

    x = inputs["x"]
    lay = _np.ascontiguousarray
    head_ones = _np.zeros((P, FB, HEADS), _np.float32)
    for h in range(HEADS):
        f, r = divmod(h * DH, P)
        head_ones[r:r + DH, f, h] = 1.0
    planes = _np.asarray(inputs["L0_attn_hyperplanes"])
    hyper = _np.zeros((HID, HEADS * BITS), planes.dtype)
    for h in range(HEADS):
        hyper[h * DH:(h + 1) * DH, h * BITS:(h + 1) * BITS] = planes[0:DH]
    powers = _np.kron(_np.eye(HEADS), 2.0 ** _np.arange(BITS)[:, None]).astype(_np.float16)
    arrays = {
        "x_t": lay(_np.reshape(x, (TOKENS, FRAME)).T),
        "w_tok": lay(_np.concatenate([_np.asarray(inputs["L0_tok_W"]).T, _np.asarray(inputs["L0_tok_b"])[None]])),
        "gamma": inputs["L0_tok_ln_gamma"],
        "beta": inputs["L0_tok_ln_beta"],
        "wq_t": lay(_np.asarray(inputs["L0_attn_Wq"]).T),
        "bq": _np.reshape(inputs["L0_attn_bq"], (FB, P)).T,
        "wv_t": lay(_np.asarray(inputs["L0_attn_Wv"]).T),
        "bv": inputs["L0_attn_bv"],
        "hyper": hyper,
        "hyper_b": _np.tile(planes[DH:].T, (HEADS, 1)),
        "base_w_t": lay(_np.asarray(inputs["L0_ffn_base_w"]).T),
        "base_b": inputs["L0_ffn_base_b"],
        "lora_a": lay(_np.reshape(_np.transpose(inputs["L0_ffn_lora_A"], (1, 0, 2)), (HID, EXPERTS * RANK))),
        "lora_b": lay(_np.reshape(inputs["L0_ffn_lora_B"], (EXPERTS * RANK, HID))),
        "router_t": lay(_np.asarray(inputs["L0_ffn_router_w"]).T),
        "router_b": inputs["L0_ffn_router_b"],
        "eye": _np.eye(P, dtype=_np.float32),
        "powers": powers,
        "head_ones": head_ones,
        "bucket_of": (_np.arange(P) % BUCKETS).astype(_np.float32)[:, None],
        "expert_rows": _np.kron(_np.eye(EXPERTS), _np.ones((1, RANK))).astype(_np.float32),
    }
    arrays = {k: lay(v) for k, v in arrays.items()}
    nc = _bacc.Bacc("TRN2", target_bir_lowering=False, num_devices=1)
    args = [nc.dram_tensor(k, v.shape, _mybir.dt.from_np(v.dtype), kind="ExternalInput").ap() for k, v in arrays.items()]
    out = nc.dram_tensor("out", (TOKENS, HID), FP32, kind="ExternalOutput").ap()
    audio_tower(nc, *args, out)
    r = _run(nc, [arrays], core_ids=[0])
    return _np.reshape(r.results[0]["out"], (BATCH, SEQ, HID))
```
